# Optimizing a Trainium2 kernel written in Bass

```python
import numpy as np
import jax
import jax.numpy as jnp

def _softmax(x, axis=-1):
    return jax.nn.softmax(x, axis=axis)

def _gelu(x):
    return jax.nn.gelu(x, approximate=True)

def _silu(x):
    return jax.nn.silu(x)

def _sigmoid(x):
    return jax.nn.sigmoid(x)

def _layernorm(x, axis=-1, eps=1e-05):
    m = jnp.mean(x, axis=axis, keepdims=True)
    v = jnp.var(x, axis=axis, keepdims=True)
    return (x - m) / jnp.sqrt(v + eps)

def _scatter_add(tgt, idx, src, axis=0):
    return tgt.at[idx].add(src)

def _segment_sum(src, seg, n):
    return jax.ops.segment_sum(src, seg, n)
kernel_name = 'mk_gnn_resnorm_d1_gnn_r8_c46abb'

def setup_inputs(seed: int=0):
    np.random.seed(seed)
    _w = jnp.asarray

    def _rec_inputs():
        import jax
        import jax.numpy as jnp
        _gk = jax.random.key(seed)
        x = -0.0007083 + 1.001 * jax.random.normal(jax.random.fold_in(_gk, 1), (6250, 48), jnp.float32)
        _s = jax.random.randint(jax.random.fold_in(_gk, 2), (100000,), 0, 6250, jnp.int32)
        _d = jax.random.randint(jax.random.fold_in(_gk, 3), (100000,), 0, 6250, jnp.int32)
        _loop = jnp.arange(6250, dtype=jnp.int32)
        src = jnp.concatenate([_s, _d, _loop])
        dst = jnp.concatenate([_d, _s, _loop])
        _o = jnp.argsort(dst, stable=True)
        src = src[_o]
        dst = dst[_o]
        edge_attr_40 = jax.random.uniform(jax.random.fold_in(_gk, 12), (206250, 40), jnp.float32, 0.0, 1)
        edge_weight = jax.random.uniform(jax.random.fold_in(_gk, 14), (206250,), jnp.float32, 0.0, 6.99999)
        node_type_119 = jax.random.randint(jax.random.fold_in(_gk, 15), (6250,), 0, 119, jnp.int32)
        node_vec = jax.random.uniform(jax.random.fold_in(_gk, 16), (6250,), jnp.float32, 0.0, 1.49999)
        return (x, src, dst, edge_attr_40, edge_weight, node_type_119, node_vec)
    x, src, dst, edge_attr_40, edge_weight, node_type_119, node_vec = _rec_inputs()

    def _L0_gnn_setup():
        import jax, jax.numpy as jnp
        import numpy as np
        CUTOFF = 6.0
        LN_EPS = 1e-05
        key = jax.random.key(seed)
        ks = jax.random.split(key, 16)
        N, E, H, R, NEL, G = (6250, 100000, 48, 40, 119, 32)
        inp = {'h': jax.random.normal(ks[0], (N, H), jnp.float32), 'edge_index': jax.random.randint(ks[1], (2, E), 0, N, jnp.int64), 'edge_attr': jax.random.uniform(ks[2], (E, R), jnp.float32), 'distances': jax.random.uniform(ks[3], (E,), jnp.float32) * 7.0, 'atom_z': jax.random.randint(ks[4], (N,), 0, NEL, jnp.int64), 'node_mult': jax.random.uniform(ks[5], (N,), jnp.float32) + 0.5, 'batch': jnp.zeros((N,), jnp.int64), 'W1': jax.random.normal(ks[6], (H, R), jnp.float32) / np.sqrt(R), 'b1': jax.random.normal(ks[7], (H,), jnp.float32) * 0.01, 'W2': jax.random.normal(ks[8], (H, H), jnp.float32) / np.sqrt(H), 'b2': jax.random.normal(ks[9], (H,), jnp.float32) * 0.01, 'emb': jax.random.normal(ks[10], (NEL, G), jnp.float32) * 0.01, 'adaptW': jax.random.normal(ks[11], (G, G), jnp.float32) * 0.01, 'gamma': jnp.ones((H,), jnp.float32), 'beta': jnp.zeros((H,), jnp.float32)}
        return inp
    _L0_gnn_all = _L0_gnn_setup()
    _L0_gnn_in = {k: v for k, v in _L0_gnn_all.items() if k in ('W1', 'b1', 'W2', 'b2', 'emb', 'adaptW', 'gamma', 'beta')}
    del _L0_gnn_all
    return {'x': x, 'src': src, 'dst': dst, 'edge_attr_40': edge_attr_40, 'edge_weight': edge_weight, 'node_type_119': node_type_119, 'node_vec': node_vec, 'L0_gnn_W1': _L0_gnn_in['W1'], 'L0_gnn_b1': _L0_gnn_in['b1'], 'L0_gnn_W2': _L0_gnn_in['W2'], 'L0_gnn_b2': _L0_gnn_in['b2'], 'L0_gnn_emb': _L0_gnn_in['emb'], 'L0_gnn_adaptW': _L0_gnn_in['adaptW'], 'L0_gnn_gamma': _L0_gnn_in['gamma'], 'L0_gnn_beta': _L0_gnn_in['beta']}

def reference(x, src, dst, edge_attr_40, edge_weight, node_type_119, node_vec, L0_gnn_W1, L0_gnn_b1, L0_gnn_W2, L0_gnn_b2, L0_gnn_emb, L0_gnn_adaptW, L0_gnn_gamma, L0_gnn_beta):
    import jax
    import jax.numpy as jnp

    def _L0_gnn_ref(h, edge_index, edge_attr, distances, atom_z, node_mult, batch, W1, b1, W2, b2, emb, adaptW, gamma, beta):
        import jax, jax.numpy as jnp
        import numpy as np
        CUTOFF = 6.0
        LN_EPS = 1e-05
        src, dst = (edge_index[0], edge_index[1])
        N = h.shape[0]
        gate = jax.nn.silu(edge_attr @ W1.T + b1) @ W2.T + b2
        ei = emb[atom_z[src]]
        ej = emb[atom_z[dst]]
        adapt_logit = jnp.sum(ei * (ej @ adaptW.T), axis=-1, keepdims=True)
        gate = gate + adapt_logit
        cw = jnp.where(distances < CUTOFF, 0.5 * (jnp.cos(jnp.pi * distances / CUTOFF) + 1.0), 0.0)
        mj = node_mult[dst]
        msg = gate * h[dst] * (cw * mj)[:, None]
        agg = jax.ops.segment_sum(msg, src, num_segments=N)
        tot = jax.ops.segment_sum(mj, src, num_segments=N)
        agg = agg / jnp.clip(tot, 1e-08, None)[:, None]
        x = h + agg
        mu = jnp.mean(x, axis=-1, keepdims=True)
        var = jnp.mean(jnp.square(x - mu), axis=-1, keepdims=True)
        return (x - mu) / jnp.sqrt(var + LN_EPS) * gamma + beta
    edge_index = jnp.stack([src, dst])
    batch0 = jnp.zeros((6250,), jnp.int32)
    x = _layernorm(x + _L0_gnn_ref(x, edge_index, edge_attr_40, edge_weight, node_type_119, node_vec, batch0, L0_gnn_W1, L0_gnn_b1, L0_gnn_W2, L0_gnn_b2, L0_gnn_emb, L0_gnn_adaptW, L0_gnn_gamma, L0_gnn_beta), axis=-1)
    return x

_drawn_inputs = setup_inputs


def setup_inputs(seed=0):
    import zlib

    import numpy as np

    out = dict(_drawn_inputs(seed))
    spreads = {'L0_gnn_gamma': (1.0, 0.2), 'L0_gnn_beta': (0.0, 0.1)}
    factors = {'edge_attr_40': 5.814,
     'edge_weight': 4.808,
     'node_vec': 6.237,
     'L0_gnn_W1': 3.434,
     'L0_gnn_b1': 64.0,
     'L0_gnn_W2': 3.268,
     'L0_gnn_b2': 200.0,
     'L0_gnn_emb': 64.0,
     'L0_gnn_adaptW': 64.0}
    for name, (base, spread) in spreads.items():
        noise = np.random.default_rng([zlib.crc32(name.encode()), seed]).standard_normal(out[name].shape)
        drawn = base * np.exp(spread * noise) if base else spread * noise
        out[name] = jnp.asarray(drawn.astype(out[name].dtype))
    for name, factor in factors.items():
        out[name] = (out[name] * factor).astype(out[name].dtype)
    return out
```

```python
import math
from contextlib import ExitStack

import concourse.bass as bass
from concourse import mybir


N, H, R, NEL, GE = 6250, 48, 40, 119, 32
E = 206250
P = 128
NB = -(-N // P)
T = 8
G = -(-E // (P * T))
EP = G * P * T
C = G * T
TBL = H + 1 + NEL
REC = H + 2
MW = H + 1
NA, NBL = 7, 8
J = 16
ZB = 7
K3 = 4
CH = EP // (P * K3)
IB = 4
IP = -(-(CH + NB + 1) // (IB * 2)) * 2
ITEMS = IB * IP
S3 = 8
CUTOFF = 6.0
EPS = 1e-5


def build(nc, x, src, dst_rows, weight, ea, z_nodes, z_row, mult_nodes,
          w1t, b1, w2t, b2, embt, adaptwt, gamma, beta, table, sorted_rec, out):
    f32, bf16 = mybir.dt.float32, mybir.dt.bfloat16
    i32, u32 = mybir.dt.int32, mybir.dt.uint32
    ALU, ACT, AX = mybir.AluOpType, mybir.ActivationFunctionType, mybir.AxisListType
    ctx = ExitStack()
    with ctx:
        def sb(name, shape, dt):
            return ctx.enter_context(nc.sbuf_tensor(name, shape, dt))

        def sem(name):
            return ctx.enter_context(nc.semaphore(name))

        bank = [ctx.enter_context(nc.psum_tensor(f"bank{i}", [P, 512], f32)) for i in range(8)]

        src_i = sb("src_i", [P, C], i32)
        hi_i = sb("hi_i", [P, C], i32)
        lo_i = sb("lo_i", [P, C], i32)
        src_f = sb("src_f", [P, C], f32)
        cutw = sb("cutw", [P, C], f32)
        dist = sb("dist", [P, C], f32)
        big1 = sb("big1", [P, NB * TBL], f32)
        big2 = sb("big2", [P, 6464], f32)
        tb = big1[:, :].rearrange("p (b c) -> p b c", c=TBL)
        iota_f = sb("iota_f", [P, P], f32)
        iota_b = sb("iota_b", [P, P], bf16)
        iota_p = sb("iota_p", [P, 1], f32)
        ident_f = sb("ident_f", [P, P], f32)
        ident_b = sb("ident_b", [P, P], bf16)
        before_b = sb("before_b", [P, P], bf16)
        ones_b = sb("ones_b", [P, P], bf16)
        ones_f = sb("ones_f", [P, P], f32)
        row_i = sb("row_i", [P, 1], i32)
        row_a = sb("row_a", [P, 2], i32)
        row_af = sb("row_af", [P, 2], f32)
        under_f = sb("under_f", [P, NBL, NB + 1], f32)
        same_j = sb("same_j", [P, J], f32)
        diag = sb("diag", [NA * J, J, NBL], f32)
        w1bd = sb("w1bd", [2 * R, 2 * H], f32)
        w2bd = sb("w2bd", [2 * H + 1, 2 * H], f32)
        b1c = sb("b1c", [2 * H, 1], f32)
        embt_s = sb("embt_s", [GE, NEL], f32)
        adwt_s = sb("adwt_s", [GE, GE], f32)
        pt_s = sb("pt_s", [GE, NEL], f32)
        at_s = sb("at_s", [NEL, NEL], f32)
        z_i = sb("z_i", [P, NB], i32)
        z_b = sb("z_b", [P, NB], bf16)
        mult_s = sb("mult_s", [P, NB], f32)
        digits = sb("digits", [NA * J, NBL], f32)
        base = sb("base", [P, NB + 1], f32)
        half_pi = sb("half_pi", [P, 1], f32)
        base_i = sb("base_i", [P, NB + 1], i32)
        first_c = sb("first_c", [P, NB], f32)
        last_c = sb("last_c", [P, NB], f32)
        tmp_i = sb("tmp_i", [P, NB], i32)
        tmp_f = sb("tmp_f", [P, NB], f32)
        ends = sb("ends", [P, NB], f32)
        shift = sb("shift", [P, NB + 1], f32)
        item_no = sb("item_no", [P, IB], f32)
        past = sb("past", [P, IB, NB], f32)
        past_d = sb("past_d", [P, IB, NB], f32)
        item_v = sb("item_v", [P, 2, IB], f32)
        item_dg = sb("item_dg", [IP, 2, IB, IP], f32)
        item_low = sb("item_low", [P, ITEMS], f32)
        item_bkt = sb("item_bkt", [1, ITEMS], i32)
        item_chk = sb("item_chk", [1, ITEMS], i32)

        ea_t = [sb(f"ea_t{u}", [P, T * R], f32) for u in range(2)]
        dst_t = [sb(f"dst_t{u}", [P, T], u32) for u in range(2)]
        row_t = [sb(f"row_t{u}", [P, T, TBL], f32) for u in range(2)]
        rec_t = [sb(f"rec_t{u}", [P, T, REC], f32) for u in range(2)]
        pos_t = [sb(f"pos_t{u}", [P, T], u32) for u in range(2)]
        eat_s = sb("eat_s", [2 * R, 512], f32)
        hid_s = sb("hid_s", [2 * H + 1, 512], f32)
        oh_hi = sb("oh_hi", [P, T, NB], bf16)
        oh_lo = sb("oh_lo", [P, T, P], bf16)
        oht_s = sb("oht_s", [P, T * P], bf16)
        picked = sb("picked", [P, T, NB], f32)
        rank_p = sb("rank_p", [P, T, NB], f32)
        zs = sb("zs", [P, T], f32)
        pos_f = sb("pos_f", [P, T], f32)
        adapt = sb("adapt", [P, T], f32)
        junk = sb("junk", [P, T, NEL], f32)
        wm = sb("wm", [P, T], f32)
        gate_s = sb("gate_s", [P, T, H], f32)
        wh_s = sb("wh_s", [P, T, H], f32)

        rec3 = [sb(f"rec3_{u}", [P, K3, REC], f32) for u in range(S3)]
        rel3 = [sb(f"rel3_{u}", [P, K3], f32) for u in range(2)]
        oh3 = [sb(f"oh3_{u}", [P, K3, P], f32) for u in range(2)]
        part3 = [sb(f"part3_{u}", [P, MW], f32) for u in range(2)]
        gam = sb("gam", [P, H], f32)
        bet = sb("bet", [P, H], f32)
        stat = [sb(f"stat{i}", [P, NB], f32) for i in range(2)]


        oh_a = big1[:, 0:C * NA // 2].bitcast(bf16).rearrange("p (g a j) -> p g a j", a=NA, j=J)
        oh_b = big2[:, 0:C * NBL // 2].bitcast(bf16).rearrange("p (g j b) -> p g j b", b=NBL, j=J)
        zrow_i = sb("zrow_i", [NEL, NB * P], i32)
        zoh = sb("zoh", [NEL, ZB * P], f32)
        sums = big1[:, 0:(NB + 1) * MW].rearrange("p (b c) -> p b c", c=MW)
        xn = big1[:, 2560:2560 + NB * H].rearrange("p (b c) -> p b c", c=H)
        y1 = big1[:, 4992:4992 + NB * H].rearrange("p (b c) -> p b c", c=H)
        y2 = big2[:, 0:NB * H].rearrange("p (b c) -> p b c", c=H)
        sq = big2[:, 2560:2560 + NB * H].rearrange("p (b c) -> p b c", c=H)

        names = """src_in dist_in consts_in z_in zrow_in x_in table_out
            pool_turn pool_step consts_ready dve_step hist_in hist_ready digits_ready base_psum
            pt_psum pt_ready at_psum at_ready zoh_ready rows_psum rows_ready mult_ready zb_ready
            dist_clip cos_ready hilo_ready w_ready
            hi_ready lo_ready rank_psum count_psum oht_psum oht_ready eat_psum eat_ready
            hid_psum hid_ready gate_psum zlook_psum z_picked zs_ready rank_picked posf_ready pos_ready
            base_moved adapt_ready gate_ready wm_ready wh_ready rec_ready side_ready
            items_diag item_psum items_ready
            rel_ready oh3_ready part_psum part_ready part_added sums_zero xn_in gb_in
            sums_done var_ready std_ready y_ready out_done""".split()
        s = {n: sem(n) for n in names}
        ea_in = [sem(f"ea_in{u}") for u in range(2)]
        dst_in = [sem(f"dst_in{u}") for u in range(2)]
        rows_in = [sem(f"rows_in{u}") for u in range(2)]
        rec_out = [sem(f"rec_out{u}") for u in range(2)]
        rec3_in = [sem(f"rec3_in{u}") for u in range(S3)]
        block = ctx.enter_context(nc.Block())

        def over_last(ap, n):
            return ap.unsqueeze(ap.ndim).to_broadcast(list(ap.shape) + [n])

        def over_mid(ap, n):
            return ap.unsqueeze(1).to_broadcast([ap.shape[0], n] + list(ap.shape[1:]))

        gate_bank = bank[2][:, 0:T * H].rearrange("p (t c) -> p t c", c=H)
        oht_bank = bank[3][:, :].bitcast(bf16)
        zlook_bank = bank[4][:, 0:T * NB].rearrange("p (t c) -> p t c", c=NB)
        rank_bank = bank[5][:, 0:T * NB].rearrange("p (t c) -> p t c", c=NB)
        HALF = G // 2

        @block.sync
        def _(sp):
            sp.dma_start(src_i[:, :], src).then_inc(s["src_in"], 16)
            sp.dma_start(zrow_i[:, :], z_row.partition_broadcast(NEL)).then_inc(s["zrow_in"], 16)
            sp.dma_start(dist[:, :], weight).then_inc(s["dist_in"], 16)
            sp.dma_start(z_i[:, :], z_nodes).then_inc(s["z_in"], 16)
            sp.dma_start(mult_s[:, :], mult_nodes).then_inc(s["z_in"], 16)
            sp.wait_ge(s["hist_ready"], 1)
            sp.dma_start(tb[:, :, 0:H], x.rearrange("(b p) c -> p b c", p=P)).then_inc(s["x_in"], 16)
            sp.wait_ge(s["x_in"], 16)
            sp.wait_ge(s["mult_ready"], 1)
            sp.wait_ge(s["rows_ready"], 2 * (NB // ZB))
            sp.dma_start(table.rearrange("(b p) c -> p b c", p=P), tb[:, :, :]).then_inc(s["table_out"], 16)

            def group(i, u, first):
                g = 2 * i + u
                if not first:
                    sp.wait_ge(s["eat_psum"], g - 1)
                sp.dma_start(ea_t[u][:, :], ea[bass.ds(g * P, P), :]).then_inc(ea_in[u], 16)
                if not first:
                    sp.wait_ge(rows_in[u], P * i)
                sp.dma_start(dst_t[u][:, :], dst_rows[bass.ds(g * P, P), :]).then_inc(dst_in[u], 16)
            group(0, 0, True)
            group(0, 1, True)
            with sp.Fori(1, HALF) as i:
                group(i, 0, False)
                group(i, 1, False)

            sp.wait_ge(s["table_out"], 16)
            sp.dma_start(xn, x.rearrange("(b p) c -> p b c", p=P)).then_inc(s["xn_in"], 16)
            sp.wait_ge(s["items_ready"], 1)
            for u in range(2):
                sp.wait_ge(rec_out[u], 16 * T * HALF)

            def chunk(i, u, first):
                j = S3 * i + u
                if not first:
                    sp.wait_ge(s["part_psum"], j - S3 + 1)
                c = sp.value_load(item_chk[0:1, bass.ds(j, 1)], min_val=0, max_val=CH - 1)
                sp.dma_start(rec3[u][:, :, :],
                             sorted_rec[bass.ds(c * (P * K3), P * K3), :]
                             .rearrange("(p t) c -> p t c", t=K3)).then_inc(rec3_in[u], 16)
            for u in range(S3):
                chunk(0, u, True)
            with sp.Fori(1, ITEMS // S3) as i:
                for u in range(S3):
                    chunk(i, u, False)

            sp.wait_ge(s["y_ready"], 1)
            full = N // P
            sp.dma_start(out[0:full * P, :].rearrange("(b p) c -> p b c", p=P),
                         y2[:, 0:full, :]).then_inc(s["out_done"], 16)
            sp.dma_start(out[full * P:N, :], y2[0:N - full * P, full, :]).then_inc(s["out_done"], 16)
            sp.wait_ge(s["out_done"], 32)

        @block.gpsimd
        def _(pool):
            step = [0]

            def link(ins):
                step[0] += 1
                ins.then_inc(s["pool_step"], 1)
                pool.wait_ge(s["pool_step"], step[0])

            def iota(t, pattern, cm):
                link(pool.iota(t, pattern, base=0, channel_multiplier=cm, allow_small_or_imprecise_dtypes=True))

            iota(iota_f[:, :], [[1, P]], 0)
            iota(iota_b[:, :], [[1, P]], 0)
            iota(iota_p[:, :], [[0, 1]], 1)
            iota(row_i[:, :], [[0, 1]], 1)
            iota(under_f[:, :, :], [[-1, NBL], [1, NB + 1]], 0)
            iota(item_no[:, :], [[IP, IB]], 1)
            link(pool.memset(ones_b[:, :], 1.0))
            link(pool.memset(ones_f[:, :], 1.0))
            link(pool.memset(hid_s[2 * H:2 * H + 1, :], 1.0))
            link(pool.memset(half_pi[:, :], math.pi / 2))
            link(pool.memset(ident_f[:, :], 0.0))
            link(pool.memset(ident_b[:, :], 0.0))
            link(pool.memset(before_b[:, :], 1.0))
            for m in (ident_f, ident_b):
                link(pool.affine_select(out=m[:, :], in_=m[:, :], compare_op=ALU.not_equal, fill=1.0,
                                        base=0, pattern=[[-1, P]], channel_multiplier=1))
            link(pool.affine_select(out=before_b[:, :], in_=before_b[:, :], compare_op=ALU.is_gt, fill=0.0,
                                    base=0, pattern=[[1, P]], channel_multiplier=-1))
            pool.memset(w1bd[:, :], 0.0).then_inc(s["consts_ready"], 1)
            pool.memset(w2bd[:, :], 0.0).then_inc(s["consts_ready"], 1)

            pool.wait_ge(s["table_out"], 16)

            def gather(i, u):
                pool.wait_ge(dst_in[u], 16 * i + 16)
                pool.sem_inc(s["pool_turn"], 1)
                for t in range(T):
                    pool.indirect_dma_start(row_t[u][:, t, :], None, table,
                                            bass.IndirectOffsetOnAxis(ap=dst_t[u][:, t:t + 1], axis=0))\
                        .then_inc(rows_in[u], 16)

            def scatter(i, u):
                g = 2 * i + u
                pool.wait_ge(s["rec_ready"], g + 1)
                pool.wait_ge(s["side_ready"], 2 * g + 2)
                pool.wait_ge(s["pos_ready"], g + 1)
                pool.sem_inc(s["pool_turn"], 1)
                for t in range(T):
                    pool.indirect_dma_start(sorted_rec, bass.IndirectOffsetOnAxis(ap=pos_t[u][:, t:t + 1], axis=0),
                                            rec_t[u][:, t, :], None).then_inc(rec_out[u], 16)

            gather(0, 0)
            gather(0, 1)
            with pool.Fori(0, HALF - 1) as i:
                scatter(i, 0)
                gather(i + 1, 0)
                scatter(i, 1)
                gather(i + 1, 1)
            scatter(HALF - 1, 0)
            scatter(HALF - 1, 1)

            pool.memset(big1[:, 0:(NB + 1) * MW], 0.0).then_inc(s["sums_zero"], 1)
            pool.wait_ge(s["sums_zero"], 1)
            pool.wait_ge(s["items_ready"], 1)

            def add_item(i, u, first):
                j = 2 * i + u
                b = pool.value_load(item_bkt[0:1, bass.ds(j, 1)], min_val=0, max_val=NB)
                pool.wait_ge(s["part_ready"], j + 1)
                if not first or u:
                    pool.wait_ge(s["part_added"], j)
                dest = big1[:, bass.ds(b * MW, MW)]
                pool.tensor_tensor(dest, dest, part3[u][:, :], ALU.add).then_inc(s["part_added"], 1)
            add_item(0, 0, True)
            add_item(0, 1, True)
            with pool.Fori(1, ITEMS // 2) as i:
                add_item(i, 0, False)
                add_item(i, 1, False)

        @block.scalar
        def _(act):
            act.wait_ge(s["consts_ready"], 2)
            for u in range(2):
                act.dma_start(w1bd[u * R:(u + 1) * R, u * H:(u + 1) * H], w1t).then_inc(s["consts_in"], 16)
                act.dma_start(w2bd[u * H:(u + 1) * H, u * H:(u + 1) * H], w2t).then_inc(s["consts_in"], 16)
                act.dma_start(b1c[u * H:(u + 1) * H, :], b1).then_inc(s["consts_in"], 16)
                act.dma_start(w2bd[2 * H:2 * H + 1, u * H:(u + 1) * H], b2).then_inc(s["consts_in"], 16)
            act.dma_start(embt_s[:, :], embt).then_inc(s["consts_in"], 16)
            act.dma_start(adwt_s[:, :], adaptwt).then_inc(s["consts_in"], 16)
            act.dma_start(gam[:, :], gamma.partition_broadcast(P)).then_inc(s["gb_in"], 16)
            act.dma_start(bet[:, :], beta.partition_broadcast(P)).then_inc(s["gb_in"], 16)
            act.wait_ge(s["pt_psum"], 1)
            act.activation(pt_s[:, :], bank[1][0:GE, 0:NEL], ACT.Copy).then_inc(s["pt_ready"], 1)
            act.wait_ge(s["at_psum"], 1)
            act.activation(at_s[:, :], bank[1][0:NEL, 128:128 + NEL], ACT.Copy).then_inc(s["at_ready"], 1)
            act.wait_ge(s["dist_clip"], 1)
            act.activation(cutw[:, :], cutw[:, :], ACT.Sin, bias=half_pi[:, :],
                           scale=-math.pi / CUTOFF).then_inc(s["cos_ready"], 1)
            act.wait_ge(s["hist_ready"], 1)
            act.wait_ge(s["z_in"], 32)
            act.activation(tb[:, :, H], mult_s[:, :], ACT.Copy).then_inc(s["mult_ready"], 1)
            with act.Fori(0, NB // ZB) as i:
                for k, (b0, nb) in enumerate(((0, 4), (4, ZB - 4))):
                    act.wait_ge(s["rows_psum"], 2 * i + k + 1)
                    act.activation(tb[:, bass.ds(i * ZB + b0, nb), H + 1:TBL],
                                   bank[2 + k][:, 0:nb * NEL].rearrange("p (b c) -> p b c", c=NEL),
                                   ACT.Copy).then_inc(s["rows_ready"], 1)

            def group(i, u, first):
                g = 2 * i + u
                prev, again = not first or u > 0, not first
                act.wait_ge(s["oht_psum"], g + 1)
                if prev:
                    act.wait_ge(s["zlook_psum"], g)
                act.activation(oht_s[:, :], oht_bank, ACT.Copy).then_inc(s["oht_ready"], 1)
                act.wait_ge(s["eat_psum"], g + 1)
                if prev:
                    act.wait_ge(s["hid_psum"], g)
                act.activation(eat_s[:, :], bank[0][0:2 * R, :], ACT.Copy).then_inc(s["eat_ready"], 1)
                act.wait_ge(s["hid_psum"], g + 1)
                if prev:
                    act.wait_ge(s["gate_psum"], g)
                act.activation(hid_s[0:2 * H, :], bank[1][0:2 * H, :], ACT.Silu,
                               bias=b1c[:, :]).then_inc(s["hid_ready"], 1)
                act.wait_ge(rows_in[u], P * i + P)
                if again:
                    act.wait_ge(rec_out[u], P * i)
                act.activation(rec_t[u][:, :, H], row_t[u][:, :, H], ACT.Copy).then_inc(s["side_ready"], 1)
                act.activation(rec_t[u][:, :, H + 1], src_f[:, bass.ds(g * T, T)], ACT.Copy)\
                    .then_inc(s["side_ready"], 1)

            act.wait_ge(s["hilo_ready"], 1)
            group(0, 0, True)
            group(0, 1, True)
            with act.Fori(1, HALF) as i:
                group(i, 0, False)
                group(i, 1, False)

            def item(i, u, first):
                j = 2 * i + u
                act.wait_ge(s["part_psum"], j + 1)
                if not first:
                    act.wait_ge(s["part_added"], j - 1)
                act.activation(part3[u][:, :], bank[u][:, 0:MW], ACT.Copy).then_inc(s["part_ready"], 1)
            item(0, 0, True)
            item(0, 1, True)
            with act.Fori(1, ITEMS // 2) as i:
                item(i, 0, False)
                item(i, 1, False)
            for n in range(2):
                act.wait_ge(s["var_ready"], n + 1)
                act.activation(stat[1][:, :], stat[0][:, :], ACT.Sqrt).then_inc(s["std_ready"], 1)

        @block.vector
        def _(dve):
            step = [0]

            def link(ins):
                step[0] += 1
                ins.then_inc(s["dve_step"], 1)
                dve.wait_ge(s["dve_step"], step[0])

            dve.wait_ge(s["src_in"], 16)
            dig_a = src_f[:, :].bitcast(i32)
            link(nc.vector.tensor_scalar(dig_a, src_i[:, :], 10, None, ALU.logical_shift_right))
            link(nc.vector.tensor_scalar(hi_i[:, :], src_i[:, :], 7, NBL - 1,
                                         ALU.logical_shift_right, ALU.bitwise_and))
            dve.wait_ge(s["consts_ready"], 2)
            link(nc.vector.tensor_tensor(
                oh_a, dig_a.rearrange("p (g j) -> p g j", j=J).unsqueeze(2).to_broadcast([P, C // J, NA, J]),
                over_last(iota_f[:, 0:NA], J).unsqueeze(1).to_broadcast([P, C // J, NA, J]), ALU.is_equal))
            link(nc.vector.tensor_tensor(
                oh_b.rearrange("p g j b -> p (g j) b"), over_last(hi_i[:, :], NBL),
                over_mid(iota_f[:, 0:NBL], C), ALU.is_equal))
            nc.vector.tensor_copy(z_b[:, 0:1], iota_f[:, 0:1]).then_inc(s["hist_in"], 1)
            link(nc.vector.tensor_scalar(hi_i[:, :], src_i[:, :], 7, None, ALU.logical_shift_right))
            link(nc.vector.tensor_scalar(lo_i[:, :], src_i[:, :], P - 1, None, ALU.bitwise_and))
            nc.vector.tensor_copy(src_f[:, :], src_i[:, :]).then_inc(s["hilo_ready"], 1)
            dve.wait_ge(s["dist_in"], 16)
            nc.vector.tensor_scalar(cutw[:, :], dist[:, :], CUTOFF, None, ALU.min).then_inc(s["dist_clip"], 1)
            link(nc.vector.tensor_scalar(row_a[:, 0:1], row_i[:, :], 4, 3,
                                         ALU.logical_shift_right, ALU.logical_shift_left))
            link(nc.vector.tensor_scalar(row_a[:, 1:2], row_i[:, :], J - 1, None, ALU.bitwise_and))
            link(nc.vector.tensor_copy(row_af[:, :], row_a[:, :]))
            link(nc.vector.tensor_scalar(under_f[:, :, :], under_f[:, :, :], row_af[:, 0:1], None, ALU.is_gt))
            link(nc.vector.tensor_scalar(same_j[:, :], iota_f[:, 0:J], row_af[:, 1:2], None, ALU.is_equal))
            dve.wait_ge(s["hist_ready"], 1)
            link(nc.vector.tensor_tensor(diag[:, :, :],
                                         bank[0][0:NA * J, 0:J * NBL].rearrange("p (j b) -> p j b", b=NBL),
                                         over_last(same_j[0:NA * J, :], NBL), ALU.mult))
            link(nc.vector.reduce_sum(digits[:, :], diag[:, :, :].rearrange("p j b -> p b j"), axis=AX.X))
            nc.vector.tensor_copy(z_b[:, 0:1], iota_f[:, 0:1]).then_inc(s["digits_ready"], 1)
            dve.wait_ge(s["base_psum"], 1)
            link(nc.vector.tensor_copy(base[:, :], bank[0][:, 256:256 + NB + 1]))
            link(nc.vector.tensor_copy(base_i[:, :], base[:, :]))

            dve.wait_ge(s["zrow_in"], 16)
            dve.wait_ge(s["z_in"], 32)
            nc.vector.tensor_copy(z_b[:, :], z_i[:, :]).then_inc(s["zb_ready"], 1)

            def types(i, first):
                if not first:
                    dve.wait_ge(s["rows_psum"], 2 * i)
                nc.vector.tensor_scalar(zoh[:, :], zrow_i[:, bass.ds(i * (ZB * P), ZB * P)], iota_p[0:NEL, :],
                                        None, ALU.is_equal).then_inc(s["zoh_ready"], 1)
            types(0, True)
            with dve.Fori(1, NB // ZB) as i:
                types(i, False)
            dve.wait_ge(s["cos_ready"], 1)
            link(nc.vector.tensor_scalar(cutw[:, :], cutw[:, :], 1.0, 0.5, ALU.add, ALU.mult))
            link(nc.vector.scalar_tensor_tensor(cutw[:, :], dist[:, :], CUTOFF, cutw[:, :],
                                                ALU.is_lt, ALU.mult))

            link(nc.vector.tensor_scalar(tmp_i[:, :], base_i[:, 0:NB], 9, None, ALU.arith_shift_right))
            link(nc.vector.tensor_scalar(first_c[:, :], tmp_i[:, :], float(CH - 1), None, ALU.min))
            link(nc.vector.tensor_scalar(tmp_f[:, :], base[:, 1:NB + 1], -1.0, None, ALU.add))
            link(nc.vector.tensor_copy(tmp_i[:, :], tmp_f[:, :]))
            link(nc.vector.tensor_scalar(tmp_i[:, :], tmp_i[:, :], 9, None, ALU.arith_shift_right))
            link(nc.vector.tensor_copy(tmp_f[:, :], tmp_i[:, :]))
            link(nc.vector.tensor_tensor(last_c[:, :], tmp_f[:, :], first_c[:, :], ALU.max))
            link(nc.vector.tensor_tensor(last_c[:, :], last_c[:, :], first_c[:, :], ALU.subtract))
            link(nc.vector.tensor_scalar(last_c[:, :], last_c[:, :], 1.0, None, ALU.add))
            link(nc.vector.tensor_tensor_scan(ends[:, :], ones_f[:, 0:NB], last_c[:, :], 0.0, ALU.mult, ALU.add))
            link(nc.vector.tensor_tensor(tmp_f[:, :], last_c[:, :], ends[:, :], ALU.subtract))
            link(nc.vector.tensor_tensor(first_c[:, :], first_c[:, :], tmp_f[:, :], ALU.add))
            link(nc.vector.memset(shift[:, :], 0.0))
            link(nc.vector.tensor_tensor(shift[:, 0:NB - 1], first_c[:, 1:NB], first_c[:, 0:NB - 1], ALU.subtract))
            link(nc.vector.tensor_tensor(past[:, :, :], over_mid(ends[:, :], IB), over_last(item_no[:, :], NB),
                                         ALU.is_le))
            link(nc.vector.tensor_tensor(past_d[:, :, :], past[:, :, :], over_mid(shift[:, 0:NB], IB), ALU.mult))
            link(nc.vector.reduce_sum(item_v[:, 0, :], past[:, :, :], axis=AX.X))
            link(nc.vector.reduce_sum(item_v[:, 1, :], past_d[:, :, :], axis=AX.X))
            link(nc.vector.tensor_tensor(item_v[:, 1, :], item_v[:, 1, :], item_no[:, :], ALU.add))
            link(nc.vector.tensor_scalar(item_v[:, 1, :], item_v[:, 1, :], float(CH - 1), None, ALU.min))
            for w in range(2):
                nc.vector.tensor_tensor(item_dg[:, w], over_last(item_v[0:IP, w, :], IP),
                                        over_mid(ident_f[0:IP, 0:IP], IB), ALU.mult).then_inc(s["items_diag"], 1)
            dve.wait_ge(s["item_psum"], 2)
            link(nc.vector.tensor_scalar(item_low[:, :], bank[6][:, 0:ITEMS], float(P), None, ALU.mult))
            nc.vector.tensor_copy(item_bkt[:, :], bank[6][0:1, 0:ITEMS]).then_inc(s["items_ready"], 1)
            nc.vector.tensor_copy(item_chk[:, :], bank[7][0:1, 0:ITEMS]).then_inc(s["items_ready"], 1)

            def group(i, u, first):
                g = 2 * i + u
                prev, again = not first or u > 0, not first
                if prev:
                    dve.wait_ge(s["count_psum"], g)
                nc.vector.tensor_tensor(oh_hi[:, :, :], over_last(hi_i[:, bass.ds(g * T, T)], NB),
                                        over_mid(iota_f[:, 0:NB], T), ALU.is_equal).then_inc(s["hi_ready"], 1)
                if prev:
                    dve.wait_ge(s["oht_psum"], g)
                nc.vector.tensor_tensor(oh_lo[:, :, :], over_last(lo_i[:, bass.ds(g * T, T)], P),
                                        over_mid(iota_f[:, :], T), ALU.is_equal).then_inc(s["lo_ready"], 1)
                dve.wait_ge(s["hi_ready"], g + 1)
                dve.wait_ge(s["rank_psum"], g + 1)
                nc.vector.tensor_tensor(rank_p[:, :, :], rank_bank, oh_hi[:, :, :], ALU.mult)\
                    .then_inc(s["rank_picked"], 1)
                dve.wait_ge(s["count_psum"], g + 1)
                nc.vector.tensor_tensor(base[:, 0:NB], base[:, 0:NB], bank[6][:, 0:NB], ALU.add)\
                    .then_inc(s["base_moved"], 1)
                dve.wait_ge(s["rank_picked"], g + 1)
                nc.vector.reduce_sum(pos_f[:, :], rank_p[:, :, :], axis=AX.X).then_inc(s["posf_ready"], 1)
                if again:
                    dve.wait_ge(rec_out[u], P * i)
                dve.wait_ge(s["posf_ready"], g + 1)
                nc.vector.tensor_copy(pos_t[u][:, :], pos_f[:, :]).then_inc(s["pos_ready"], 1)
                dve.wait_ge(s["zlook_psum"], g + 1)
                nc.vector.tensor_tensor(picked[:, :, :], zlook_bank, oh_hi[:, :, :], ALU.mult)\
                    .then_inc(s["z_picked"], 1)
                dve.wait_ge(s["z_picked"], g + 1)
                nc.vector.reduce_sum(zs[:, :], picked[:, :, :], axis=AX.X).then_inc(s["zs_ready"], 1)
                dve.wait_ge(rows_in[u], P * i + P)
                dve.wait_ge(s["zs_ready"], g + 1)
                for t in range(T):
                    nc.vector.scalar_tensor_tensor(junk[:, t, :], iota_f[:, 0:NEL], zs[:, t:t + 1],
                                                   row_t[u][:, t, H + 1:TBL], ALU.is_equal, ALU.mult,
                                                   accum_out=adapt[:, t:t + 1]).then_inc(s["adapt_ready"], 1)
                nc.vector.tensor_tensor(wm[:, :], row_t[u][:, :, H], cutw[:, bass.ds(g * T, T)], ALU.mult)\
                    .then_inc(s["wm_ready"], 1)
                dve.wait_ge(s["gate_psum"], g + 1)
                dve.wait_ge(s["adapt_ready"], T * g + T)
                nc.vector.tensor_tensor(gate_s[:, :, :], gate_bank, over_last(adapt[:, :], H), ALU.add)\
                    .then_inc(s["gate_ready"], 1)
                dve.wait_ge(s["wm_ready"], g + 1)
                nc.vector.tensor_tensor(wh_s[:, :, :], row_t[u][:, :, 0:H], over_last(wm[:, :], H), ALU.mult)\
                    .then_inc(s["wh_ready"], 1)
                dve.wait_ge(s["gate_ready"], g + 1)
                dve.wait_ge(s["wh_ready"], g + 1)
                nc.vector.tensor_tensor(rec_t[u][:, :, 0:H], gate_s[:, :, :], wh_s[:, :, :], ALU.mult)\
                    .then_inc(s["rec_ready"], 1)
            group(0, 0, True)
            group(0, 1, True)
            with dve.Fori(1, HALF) as i:
                group(i, 0, False)
                group(i, 1, False)

            def item(i, u, first):
                j = S3 * i + u
                v = u % 2
                dve.wait_ge(rec3_in[u], 16 * i + 16)
                if not first or u >= 2:
                    dve.wait_ge(s["part_psum"], j - 1)
                nc.vector.tensor_scalar(rel3[v][:, :], rec3[u][:, :, H + 1], item_low[:, bass.ds(j, 1)], None,
                                        ALU.subtract).then_inc(s["rel_ready"], 1)
                dve.wait_ge(s["rel_ready"], j + 1)
                nc.vector.tensor_tensor(oh3[v][:, :, :], over_mid(iota_f[:, :], K3), over_last(rel3[v][:, :], P),
                                        ALU.is_equal).then_inc(s["oh3_ready"], 1)
            for u in range(S3):
                item(0, u, True)
            with dve.Fori(1, ITEMS // S3) as i:
                for u in range(S3):
                    item(i, u, False)

            dve.wait_ge(s["part_added"], ITEMS)
            dve.wait_ge(s["xn_in"], 16)
            dve.wait_ge(s["gb_in"], 32)
            link(nc.vector.tensor_scalar(stat[0][:, :], sums[:, 0:NB, H], 1e-8, None, ALU.max))
            link(nc.vector.reciprocal(stat[1][:, :], stat[0][:, :]))
            link(nc.vector.tensor_tensor(y1, sums[:, 0:NB, 0:H], over_last(stat[1][:, :], H), ALU.mult))
            link(nc.vector.tensor_tensor(y1, y1, xn, ALU.add))

            def norm(y, n):
                link(nc.vector.reduce_sum(stat[0][:, :], y, axis=AX.X))
                link(nc.vector.tensor_scalar(stat[0][:, :], stat[0][:, :], 1.0 / H, None, ALU.mult))
                link(nc.vector.tensor_tensor(y, y, over_last(stat[0][:, :], H), ALU.subtract))
                link(nc.vector.tensor_tensor(sq, y, y, ALU.mult))
                link(nc.vector.reduce_sum(stat[0][:, :], sq, axis=AX.X))
                nc.vector.tensor_scalar(stat[0][:, :], stat[0][:, :], 1.0 / H, EPS, ALU.mult, ALU.add)\
                    .then_inc(s["var_ready"], 1)
                dve.wait_ge(s["std_ready"], n + 1)
                link(nc.vector.reciprocal(stat[0][:, :], stat[1][:, :]))
            norm(y1, 0)
            link(nc.vector.tensor_tensor(y1, y1, over_last(stat[0][:, :], H), ALU.mult))
            link(nc.vector.tensor_tensor(y1, y1, over_mid(gam[:, :], NB), ALU.mult))
            link(nc.vector.tensor_tensor(y1, y1, over_mid(bet[:, :], NB), ALU.add))
            link(nc.vector.tensor_tensor(y1, y1, xn, ALU.add))
            norm(y1, 1)
            nc.vector.tensor_tensor(y2, y1, over_last(stat[0][:, :], H), ALU.mult).then_inc(s["y_ready"], 1)

        @block.tensor
        def _(pe):
            pe.wait_ge(s["consts_in"], 16 * 10)
            nc.tensor.matmul(bank[1][0:GE, 0:NEL], adwt_s[:, :], embt_s[:, :], start=True, stop=True)\
                .then_inc(s["pt_psum"], 1)
            pe.wait_ge(s["pt_ready"], 1)
            nc.tensor.matmul(bank[1][0:NEL, 128:128 + NEL], pt_s[:, :], embt_s[:, :], start=True, stop=True)\
                .then_inc(s["at_psum"], 1)
            pe.wait_ge(s["hist_in"], 1)
            hist = bank[0][0:NA * J, 0:J * NBL]

            def count(c, start, stop):
                return nc.tensor.matmul(hist, oh_a[:, c, :, :].rearrange("p a j -> p (a j)"),
                                        oh_b[:, c, :, :].rearrange("p j b -> p (j b)"), start=start, stop=stop)
            for c in range(C // J):
                last = count(c, c == 0, c == C // J - 1)
            last.then_inc(s["hist_ready"], 1)
            pe.wait_ge(s["digits_ready"], 1)
            for b in range(NBL):
                last = nc.tensor.matmul(bank[0][:, 256:256 + NB + 1],
                                        digits[:, b:b + 1].to_broadcast([NA * J, P]), under_f[0:NA * J, b, :],
                                        start=b == 0, stop=b == NBL - 1)
            last.then_inc(s["base_psum"], 1)
            pe.wait_ge(s["at_ready"], 1)

            def types(i, first):
                pe.wait_ge(s["zoh_ready"], i + 1)
                for k, (b0, nb) in enumerate(((0, 4), (4, ZB - 4))):
                    if not first:
                        pe.wait_ge(s["rows_ready"], 2 * i + k - 1)
                    for b in range(nb):
                        last = nc.tensor.matmul(bank[2 + k][:, b * NEL:(b + 1) * NEL],
                                                zoh[:, (b0 + b) * P:(b0 + b + 1) * P], at_s[:, :],
                                                start=True, stop=True)
                    last.then_inc(s["rows_psum"], 1)
            types(0, True)
            with pe.Fori(1, NB // ZB) as i:
                types(i, False)
            for w in range(2):
                pe.wait_ge(s["items_diag"], w + 1)
                nc.tensor.matmul(bank[6 + w][:, 0:ITEMS], ones_f[0:IP, :],
                                 item_dg[:, w].rearrange("p b c -> p (b c)"), start=True, stop=True)\
                    .then_inc(s["item_psum"], 1)
            pe.wait_ge(s["items_ready"], 2)
            pe.wait_ge(s["zb_ready"], 1)
            pe.wait_ge(s["rows_ready"], 2 * (NB // ZB))

            def group(i, u, first):
                g = 2 * i + u
                prev = not first or u > 0
                pe.wait_ge(s["hi_ready"], g + 1)
                if prev:
                    pe.wait_ge(s["base_moved"], g)
                    pe.wait_ge(s["rank_picked"], g)
                nc.tensor.matmul(rank_bank, ident_f[:, :], over_mid(base[:, 0:NB], T), start=True, stop=False,
                                 skip_group_check=True)
                last = nc.tensor.matmul(rank_bank, before_b[:, :], oh_hi[:, :, :], start=False, stop=False,
                                        skip_group_check=True)
                for t in range(T - 1):
                    last = nc.tensor.matmul(rank_bank[:, t + 1:T, :], ones_b[:, :],
                                            over_mid(oh_hi[:, t, :], T - 1 - t), start=False, stop=t == T - 2,
                                            skip_group_check=True)
                last.then_inc(s["rank_psum"], 1)
                for t in range(T):
                    last = nc.tensor.matmul(bank[6][:, 0:NB], ones_b[:, :], oh_hi[:, t, :],
                                            start=t == 0, stop=t == T - 1)
                last.then_inc(s["count_psum"], 1)
                pe.wait_ge(s["lo_ready"], g + 1)
                if prev:
                    pe.wait_ge(s["oht_ready"], g)
                for t in range(T):
                    last = nc.tensor.transpose(oht_bank[:, t * P:(t + 1) * P], oh_lo[:, t, :], ident_b[:, :])
                last.then_inc(s["oht_psum"], 1)
                pe.wait_ge(ea_in[u], 16 * i + 16)
                if prev:
                    pe.wait_ge(s["eat_ready"], g)
                for k in range(T // 2):
                    last = nc.tensor.transpose(bank[0][0:2 * R, k * P:(k + 1) * P],
                                               ea_t[u][:, 2 * R * k:2 * R * (k + 1)], ident_f[:, :])
                last.then_inc(s["eat_psum"], 1)
                pe.wait_ge(s["oht_ready"], g + 1)
                if prev:
                    pe.wait_ge(s["z_picked"], g)
                for t in range(T):
                    last = nc.tensor.matmul(zlook_bank[:, t, :], oht_s[:, t * P:(t + 1) * P], z_b[:, :],
                                            start=True, stop=True)
                last.then_inc(s["zlook_psum"], 1)
                pe.wait_ge(s["eat_ready"], g + 1)
                if prev:
                    pe.wait_ge(s["hid_ready"], g)
                nc.tensor.matmul(bank[1][0:2 * H, :], w1bd[:, :], eat_s[:, :], start=True, stop=True)\
                    .then_inc(s["hid_psum"], 1)
                pe.wait_ge(s["hid_ready"], g + 1)
                if prev:
                    pe.wait_ge(s["gate_ready"], g)
                for k in range(T // 2):
                    last = nc.tensor.matmul(bank[2][:, 2 * H * k:2 * H * (k + 1)], hid_s[:, k * P:(k + 1) * P],
                                            w2bd[:, :], start=True, stop=True)
                last.then_inc(s["gate_psum"], 1)
            group(0, 0, True)
            group(0, 1, True)
            with pe.Fori(1, HALF) as i:
                group(i, 0, False)
                group(i, 1, False)

            def item(i, u, first):
                j = S3 * i + u
                v = u % 2
                pe.wait_ge(s["oh3_ready"], j + 1)
                if not first or u >= 2:
                    pe.wait_ge(s["part_ready"], j - 1)
                for t in range(K3):
                    last = nc.tensor.matmul(bank[v][:, 0:MW], oh3[v][:, t, :], rec3[u][:, t, 0:MW],
                                            start=t == 0, stop=t == K3 - 1)
                last.then_inc(s["part_psum"], 1)
            for u in range(S3):
                item(0, u, True)
            with pe.Fori(1, ITEMS // S3) as i:
                for u in range(S3):
                    item(i, u, False)


def kernel(x, src, dst, edge_attr_40, edge_weight, node_type_119, node_vec, L0_gnn_W1, L0_gnn_b1,
           L0_gnn_W2, L0_gnn_b2, L0_gnn_emb, L0_gnn_adaptW, L0_gnn_gamma, L0_gnn_beta):
    import numpy as np
    import concourse.bacc as bacc
    from concourse.bass_utils import run_bass_kernel_spmd as run

    nc = bacc.Bacc("TRN2", target_bir_lowering=False, num_devices=1)
    pad = EP - E
    npad = NB * P - N

    def edges(a, fill):
        a = np.concatenate([np.asarray(a), np.full((pad,), fill, a.dtype)])
        return np.ascontiguousarray(a.reshape(G, P, T).transpose(1, 0, 2).reshape(P, C))

    def nodes(a):
        return np.ascontiguousarray(np.concatenate([np.asarray(a), np.zeros((npad,), a.dtype)]))

    arrays = {
        "in_x": np.concatenate([np.asarray(x), np.zeros((npad, H), np.float32)]),
        "in_src": edges(src, NB * P - 1),
        "in_dst": np.concatenate([np.asarray(dst), np.full((pad,), N - 1, np.int32)]).reshape(G * P, T),
        "in_weight": edges(edge_weight, 0),
        "in_ea": np.concatenate([np.asarray(edge_attr_40), np.zeros((pad, R), np.float32)]).reshape(G * P, T * R),
        "in_z_nodes": np.ascontiguousarray(nodes(node_type_119).reshape(NB, P).T),
        "in_z_row": nodes(node_type_119),
        "in_mult": np.ascontiguousarray(nodes(node_vec).reshape(NB, P).T),
        "in_w1t": np.ascontiguousarray(np.asarray(L0_gnn_W1).T),
        "in_b1": np.asarray(L0_gnn_b1).reshape(H, 1),
        "in_w2t": np.ascontiguousarray(np.asarray(L0_gnn_W2).T),
        "in_b2": np.asarray(L0_gnn_b2).reshape(1, H),
        "in_embt": np.ascontiguousarray(np.asarray(L0_gnn_emb).T),
        "in_adaptwt": np.ascontiguousarray(np.asarray(L0_gnn_adaptW).T),
        "in_gamma": np.asarray(L0_gnn_gamma),
        "in_beta": np.asarray(L0_gnn_beta),
    }
    args = []
    for name, a in arrays.items():
        dt = mybir.dt.from_np(a.dtype)
        if name == "in_dst":
            dt = mybir.dt.uint32
            arrays[name] = a.view(np.uint32)
        args.append(nc.dram_tensor(name, a.shape, dt, kind="ExternalInput").ap())
    args.append(nc.dram_tensor("node_table", (NB * P, TBL), mybir.dt.float32, kind="Internal").ap())
    args.append(nc.dram_tensor("sorted_rec", (EP, REC), mybir.dt.float32, kind="Internal").ap())
    args.append(nc.dram_tensor("out", (N, H), mybir.dt.float32, kind="ExternalOutput").ap())
    build(nc, *args)
    return run(nc, [arrays], core_ids=[0]).results[0]["out"]
```

```python
import math
from contextlib import ExitStack

import concourse.bass as bass
from concourse import mybir


N, H, R, NEL, GE = 6250, 48, 40, 119, 32
E = 206250
P = 128
NB = -(-N // P)
T = 8
G = -(-E // (P * T))
EP = G * P * T
C = G * T
TBL = H + 1 + NEL
REC = H + 2
MW = H + 1
NA, NBL = 7, 8
J = 16
ZB = 7
K3 = 4
CH = EP // (P * K3)
IB = 4
IP = -(-(CH + NB + 1) // (IB * 2)) * 2
GB, GP = 2, G // 2
ZSHIFT, ZBIAS = 18, 64
ITEMS = IB * IP
S3 = 8
CUTOFF = 6.0
EPS = 1e-5


def build(nc, x, src, dst, dst_rows, weight, ea, z_nodes, z_row, mult_nodes,
          w1t, b1, w2t, b2, embt, adaptwt, gamma, beta, table, sorted_rec, out):
    f32, bf16 = mybir.dt.float32, mybir.dt.bfloat16
    i32, u32 = mybir.dt.int32, mybir.dt.uint32
    ALU, ACT, AX = mybir.AluOpType, mybir.ActivationFunctionType, mybir.AxisListType
    ctx = ExitStack()
    with ctx:
        def sb(name, shape, dt):
            return ctx.enter_context(nc.sbuf_tensor(name, shape, dt))

        def sem(name):
            return ctx.enter_context(nc.semaphore(name))

        bank4 = ctx.enter_context(nc.psum_tensor("banks0_3", [P, 4 * 512], f32))
        bank = [bank4[:, 512 * i:512 * (i + 1)] for i in range(4)] +\
            [ctx.enter_context(nc.psum_tensor(f"bank{i}", [P, 512], f32)) for i in range(4, 8)]

        src_i = sb("src_i", [P, C], i32)
        hi_i = sb("hi_i", [P, C], i32)
        lo_i = sb("lo_i", [P, C], i32)
        src_f = sb("src_f", [P, C], f32)
        dst_i = sb("dst_i", [P, C], i32)
        loc = sb("loc", [P, C], f32)
        cutw = sb("cutw", [P, C], f32)
        big1 = sb("big1", [P, NB * 3 * TBL // 2], f32)
        big2 = sb("big2", [P, 6464], f32)
        tb = big1[:, :].bitcast(bf16).rearrange("p (b k c) -> p b k c", k=3, c=TBL)
        iota_f = sb("iota_f", [P, P], f32)
        iota_b = sb("iota_b", [P, P], bf16)
        iota_p = sb("iota_p", [P, 1], f32)
        ident_f = sb("ident_f", [P, P], f32)
        ident_b = sb("ident_b", [P, P], bf16)
        before_b = sb("before_b", [P, P], bf16)
        ones_b = sb("ones_b", [P, P], bf16)
        ones_f = sb("ones_f", [P, P], f32)
        row_i = sb("row_i", [P, 1], i32)
        row_a = sb("row_a", [P, 2], i32)
        row_af = sb("row_af", [P, 2], f32)
        under_f = sb("under_f", [P, NBL, NB + 1], f32)
        same_j = sb("same_j", [P, J], f32)
        diag = sb("diag", [NA * J, J, NBL], f32)
        w1bd = sb("w1bd", [2 * R, 2 * H], f32)
        w2bd = sb("w2bd", [2 * H + 1, 2 * H], f32)
        b1c = sb("b1c", [2 * H, 1], f32)
        embt_s = sb("embt_s", [GE, NEL], f32)
        adwt_s = sb("adwt_s", [GE, GE], f32)
        pt_s = sb("pt_s", [GE, NEL], f32)
        at_s = sb("at_s", [NEL, NEL], f32)
        z_i = sb("z_i", [P, NB], i32)
        z_b = sb("z_b", [P, NB], bf16)
        z_f = sb("z_f", [P, NB], f32)
        at_r = sb("at_r", [NEL, NEL], f32)
        at3 = sb("at3", [NEL, 3, NEL], bf16)
        low_g = sb("low_g", [GP, GB], f32)
        high_g = sb("high_g", [GP, GB], f32)
        fits = sb("fits", [GP, GB], f32)
        low_dg = sb("low_dg", [GP, GB, GP], f32)
        fit_all = sb("fit_all", [P, 2], f32)
        low_all = sb("low_all", [P, G], f32)
        low_i = sb("low_i", [1, G], i32)
        windowed = sb("windowed", [1, 1], i32)
        mult_s = sb("mult_s", [P, NB], f32)
        digits = sb("digits", [NA * J, NBL], f32)
        base = sb("base", [P, NB + 1], f32)
        half_pi = sb("half_pi", [P, 1], f32)
        base_i = sb("base_i", [P, NB + 1], i32)
        first_c = sb("first_c", [P, NB], f32)
        last_c = sb("last_c", [P, NB], f32)
        tmp_i = sb("tmp_i", [P, NB], i32)
        tmp_f = sb("tmp_f", [P, NB], f32)
        ends = sb("ends", [P, NB], f32)
        shift = sb("shift", [P, NB + 1], f32)
        item_no = sb("item_no", [P, IB], f32)
        past = sb("past", [P, IB, NB], f32)
        past_d = sb("past_d", [P, IB, NB], f32)
        item_v = sb("item_v", [P, 2, IB], f32)
        item_dg = sb("item_dg", [IP, 2, IB, IP], f32)
        item_low = sb("item_low", [P, ITEMS], f32)
        item_bkt = sb("item_bkt", [1, ITEMS], i32)
        item_chk = sb("item_chk", [1, ITEMS], i32)

        ea_t = [sb(f"ea_t{u}", [P, T * R], f32) for u in range(2)]
        dst_t = [sb(f"dst_t{u}", [P, T], u32) for u in range(2)]
        rec_t = [sb(f"rec_t{u}", [P, T, REC], f32) for u in range(2)]
        pos_t = [sb(f"pos_t{u}", [P, T], u32) for u in range(2)]
        eat_s = sb("eat_s", [2 * R, 512], f32)
        hid_s = sb("hid_s", [2 * H + 1, 512], f32)
        oh_hi = sb("oh_hi", [P, T, NB], bf16)
        picked = sb("picked", [P, T, NB], f32)
        place_f = sb("place_f", [P, T], f32)
        place_i = sb("place_i", [P, T], i32)
        z_edge = sb("z_edge", [P, T], i32)
        zs = sb("zs", [P, T], f32)
        adapt = sb("adapt", [P, T], f32)
        junk = sb("junk", [P, T, NEL], f32)
        wm = sb("wm", [P, T], f32)
        gate_s = sb("gate_s", [P, T, H], f32)
        wh_s = sb("wh_s", [P, T, H], f32)

        rec3 = [sb(f"rec3_{u}", [P, K3, REC], f32) for u in range(S3)]
        rel3 = [sb(f"rel3_{u}", [P, K3], f32) for u in range(2)]
        oh3 = [sb(f"oh3_{u}", [P, K3, P], f32) for u in range(2)]
        part3 = [sb(f"part3_{u}", [P, MW], f32) for u in range(2)]
        gam = sb("gam", [P, H], f32)
        bet = sb("bet", [P, H], f32)
        stat = [sb(f"stat{i}", [P, NB], f32) for i in range(2)]


        oh_a = big1[:, 0:C * NA // 2].bitcast(bf16).rearrange("p (g a j) -> p g a j", a=NA, j=J)
        oh_b = big2[:, 0:C * NBL // 2].bitcast(bf16).rearrange("p (g j b) -> p g j b", b=NBL, j=J)
        work = sb("work", [P, NB * P], f32)
        zrow_i = work[0:NEL, :].bitcast(i32)
        WW, WO = T * 3 * TBL // 2, T * P // 2
        win_t = [work[:, u * WW:(u + 1) * WW].bitcast(bf16).rearrange("p (t c) -> p t c", t=T) for u in range(2)]
        oh_lo, oh_loc, lot_s, loct_s = (work[:, 2 * WW + u * WO:2 * WW + (u + 1) * WO].bitcast(bf16)
                                        for u in range(4))
        oh_lo, oh_loc = (a.rearrange("p (t c) -> p t c", t=T) for a in (oh_lo, oh_loc))
        dist = loc
        dst_g = big1[0:GP, 8192:8192 + GB * P * T].bitcast(i32).rearrange("p (b e) -> p b e", b=GB)
        zoh = sb("zoh", [NEL, ZB * P], bf16)
        xm = big2[:, 0:NB * MW].rearrange("p (b c) -> p b c", c=MW)
        xm_r = big2[:, 2560:2560 + NB * MW].rearrange("p (b c) -> p b c", c=MW)
        sums = big1[:, 0:(NB + 1) * MW].rearrange("p (b c) -> p b c", c=MW)
        xn = big1[:, 2560:2560 + NB * H].rearrange("p (b c) -> p b c", c=H)
        y1 = big1[:, 4992:4992 + NB * H].rearrange("p (b c) -> p b c", c=H)
        y2 = big2[:, 0:NB * H].rearrange("p (b c) -> p b c", c=H)
        sq = big2[:, 2560:2560 + NB * H].rearrange("p (b c) -> p b c", c=H)

        names = """src_in dist_in consts_in z_in zrow_in x_in dst_in dstg_in table_out
            pool_turn pool_step consts_ready dve_step hist_in hist_ready digits_ready base_psum
            pt_psum pt_ready at_psum at_ready at3_ready zoh_ready rows_psum rows_ready xm_ready split_step split_ready
            zb_ready dist_clip cos_ready cut_half cutw_ready hilo_ready low_ready low_psum windows_ready
            hi_ready lo_ready loc_ready place_psum place_picked place_f_ready place_i_ready pos_ready
            z_ready zs_ready base_moved lot_psum lot_ready loct_psum loct_ready eat_psum eat_ready
            hid_psum hid_ready gate_psum gate_ready win_psum win_read adapt_ready wm_ready wh_ready
            rec_ready side_ready items_diag item_psum items_ready
            rel_ready oh3_ready part_psum part_ready part_added sums_zero xn_in gb_in
            var_ready std_ready y_ready out_done""".split()
        s = {n: sem(n) for n in names}
        ea_in = [sem(f"ea_in{u}") for u in range(2)]
        idx_in = [sem(f"idx_in{u}") for u in range(2)]
        win_in = [sem(f"win_in{u}") for u in range(2)]
        rows_in = [sem(f"rows_in{u}") for u in range(2)]
        rec_out = [sem(f"rec_out{u}") for u in range(2)]
        rec3_in = [sem(f"rec3_in{u}") for u in range(S3)]
        block = ctx.enter_context(nc.Block())

        def over_last(ap, n):
            return ap.unsqueeze(ap.ndim).to_broadcast(list(ap.shape) + [n])

        def over_mid(ap, n):
            return ap.unsqueeze(1).to_broadcast([ap.shape[0], n] + list(ap.shape[1:]))

        win_bank = bank4[:, :].rearrange("p (k c) -> p k c", k=T // 2)[:, :, 0:2 * TBL]\
            .rearrange("p k (t c) -> p k t c", t=2)
        mlp_bank, gate_psum, oht_psum, place_psum = bank[4], bank[5], bank[6], bank[7]
        gate_bank = gate_psum[:, 0:T * H].rearrange("p (t c) -> p t c", c=H)
        oht_bank = oht_psum[:, :].bitcast(bf16)
        place_bank = place_psum[:, 0:T * NB].rearrange("p (t c) -> p t c", c=NB)
        count_bank = place_psum[:, T * NB:(T + 1) * NB]
        HALF = G // 2

        @block.sync
        def _(sp):
            sp.dma_start(src_i[:, :], src).then_inc(s["src_in"], 16)
            sp.dma_start(dst_g, dst_rows.rearrange("(b g p) t -> g b (p t)", b=GB, p=P).bitcast(i32))\
                .then_inc(s["dstg_in"], 16)
            sp.dma_start(z_i[:, :], z_nodes).then_inc(s["z_in"], 16)
            sp.dma_start(mult_s[:, :], mult_nodes).then_inc(s["z_in"], 16)
            sp.dma_start(dist[:, :], weight).then_inc(s["dist_in"], 16)
            sp.dma_start(zrow_i, z_row.partition_broadcast(NEL)).then_inc(s["zrow_in"], 16)
            sp.dma_start(dst_i[:, :], dst).then_inc(s["dst_in"], 16)
            sp.wait_ge(s["hist_ready"], 1)
            sp.dma_start(xm[:, :, 0:H], x.rearrange("(b p) c -> p b c", p=P)).then_inc(s["x_in"], 16)
            sp.wait_ge(s["rows_ready"], NB)
            sp.wait_ge(s["split_ready"], 1)
            sp.dma_start(table.rearrange("(b p) c -> p b c", p=P),
                         tb.rearrange("p b k c -> p b (k c)")).then_inc(s["table_out"], 16)
            sp.wait_ge(s["table_out"], 16)

            def group(i, u, first, low):
                g = 2 * i + u
                if not first:
                    sp.wait_ge(s["eat_psum"], g - 1)
                sp.dma_start(ea_t[u][:, :], ea[bass.ds(g * P, P), :]).then_inc(ea_in[u], 16)
                if low is not None:
                    if not first:
                        sp.wait_ge(s["win_psum"], g - 1)
                    sp.dma_start(win_t[u][:, 0, :], table[bass.ds(low, P), :]).then_inc(win_in[u], 16)
                else:
                    if not first:
                        sp.wait_ge(rows_in[u], P * i)
                    sp.dma_start(dst_t[u][:, :], dst_rows[bass.ds(g * P, P), :]).then_inc(idx_in[u], 16)

            def lows(i):
                return [sp.value_load(low_i[0:1, bass.ds(2 * i + u, 1)], min_val=0, max_val=(NB - 1) * P)
                        for u in range(2)]

            sp.wait_ge(s["windows_ready"], 3)
            fast = sp.value_load(windowed[0:1, 0:1], min_val=0, max_val=1)
            with sp.If(fast > 0):
                for u, low in enumerate(lows(0)):
                    group(0, u, True, low)
                with sp.Fori(1, HALF) as i:
                    for u, low in enumerate(lows(i)):
                        group(i, u, False, low)
            with sp.Else():
                for u in range(2):
                    group(0, u, True, None)
                with sp.Fori(1, HALF) as i:
                    for u in range(2):
                        group(i, u, False, None)

            sp.wait_ge(s["table_out"], 16)
            sp.dma_start(xn, x.rearrange("(b p) c -> p b c", p=P)).then_inc(s["xn_in"], 16)
            sp.wait_ge(s["items_ready"], 1)
            for u in range(2):
                sp.wait_ge(rec_out[u], 16 * T * HALF)

            def chunks(i):
                return [sp.value_load(item_chk[0:1, bass.ds(S3 * i + u, 1)], min_val=0, max_val=CH - 1)
                        for u in range(S3)]

            def chunk(i, u, first, c):
                j = S3 * i + u
                if not first:
                    sp.wait_ge(s["part_psum"], j - S3 + 1)
                sp.dma_start(rec3[u][:, :, :],
                             sorted_rec[bass.ds(c * (P * K3), P * K3), :]
                             .rearrange("(p t) c -> p t c", t=K3)).then_inc(rec3_in[u], 16)
            for u, c in enumerate(chunks(0)):
                chunk(0, u, True, c)
            with sp.Fori(1, ITEMS // S3) as i:
                for u, c in enumerate(chunks(i)):
                    chunk(i, u, False, c)

            sp.wait_ge(s["y_ready"], 1)
            full = N // P
            sp.dma_start(out[0:full * P, :].rearrange("(b p) c -> p b c", p=P),
                         y2[:, 0:full, :]).then_inc(s["out_done"], 16)
            sp.dma_start(out[full * P:N, :], y2[0:N - full * P, full, :]).then_inc(s["out_done"], 16)
            sp.wait_ge(s["out_done"], 32)

        @block.gpsimd
        def _(pool):
            step = [0]

            def link(ins):
                step[0] += 1
                ins.then_inc(s["pool_step"], 1)
                pool.wait_ge(s["pool_step"], step[0])

            def iota(t, pattern, cm):
                link(pool.iota(t, pattern, base=0, channel_multiplier=cm, allow_small_or_imprecise_dtypes=True))

            iota(iota_f[:, :], [[1, P]], 0)
            iota(iota_b[:, :], [[1, P]], 0)
            iota(iota_p[:, :], [[0, 1]], 1)
            iota(row_i[:, :], [[0, 1]], 1)
            iota(under_f[:, :, :], [[-1, NBL], [1, NB + 1]], 0)
            iota(item_no[:, :], [[IP, IB]], 1)
            link(pool.memset(ones_b[:, :], 1.0))
            link(pool.memset(ones_f[:, :], 1.0))
            link(pool.memset(hid_s[2 * H:2 * H + 1, :], 1.0))
            link(pool.memset(half_pi[:, :], math.pi / 2))
            link(pool.memset(ident_f[:, :], 0.0))
            link(pool.memset(ident_b[:, :], 0.0))
            link(pool.memset(before_b[:, :], 1.0))
            for m in (ident_f, ident_b):
                link(pool.affine_select(out=m[:, :], in_=m[:, :], compare_op=ALU.not_equal, fill=1.0,
                                        base=0, pattern=[[-1, P]], channel_multiplier=1))
            link(pool.affine_select(out=before_b[:, :], in_=before_b[:, :], compare_op=ALU.is_gt, fill=0.0,
                                    base=0, pattern=[[1, P]], channel_multiplier=-1))
            pool.memset(w1bd[:, :], 0.0).then_inc(s["consts_ready"], 1)
            pool.memset(w2bd[:, :], 0.0).then_inc(s["consts_ready"], 1)

            pool.wait_ge(s["x_in"], 16)
            pool.wait_ge(s["z_in"], 32)
            pool.wait_ge(s["digits_ready"], 1)
            pool.wait_ge(s["low_ready"], 1)
            part = [tb[:, :, k, 0:MW] for k in range(3)]
            link(pool.tensor_copy(xm[:, :, H], mult_s[:, :]))
            link(pool.tensor_copy(part[0], xm))
            link(pool.tensor_tensor(xm_r, xm, part[0], ALU.subtract))
            link(pool.tensor_copy(part[1], xm_r))
            link(pool.tensor_tensor(xm_r, xm_r, part[1], ALU.subtract))
            pool.tensor_copy(part[2], xm_r).then_inc(s["split_ready"], 1)

            def gather(i, u):
                pool.wait_ge(idx_in[u], 16 * i + 16)
                pool.sem_inc(s["pool_turn"], 1)
                for t in range(T):
                    pool.indirect_dma_start(win_t[u][:, t, :], None, table,
                                            bass.IndirectOffsetOnAxis(ap=dst_t[u][:, t:t + 1], axis=0))\
                        .then_inc(rows_in[u], 16)

            def scatter(i, u):
                g = 2 * i + u
                pool.wait_ge(s["rec_ready"], g + 1)
                pool.wait_ge(s["side_ready"], g + 1)
                pool.wait_ge(s["pos_ready"], g + 1)
                pool.sem_inc(s["pool_turn"], 1)
                for t in range(T):
                    pool.indirect_dma_start(sorted_rec, bass.IndirectOffsetOnAxis(ap=pos_t[u][:, t:t + 1], axis=0),
                                            rec_t[u][:, t, :], None).then_inc(rec_out[u], 16)

            pool.wait_ge(s["windows_ready"], 3)
            pool.wait_ge(s["table_out"], 16)
            fast = pool.value_load(windowed[0:1, 0:1], min_val=0, max_val=1)
            with pool.If(fast > 0):
                with pool.Fori(0, HALF) as i:
                    scatter(i, 0)
                    scatter(i, 1)
            with pool.Else():
                gather(0, 0)
                gather(0, 1)
                with pool.Fori(0, HALF - 1) as i:
                    scatter(i, 0)
                    gather(i + 1, 0)
                    scatter(i, 1)
                    gather(i + 1, 1)
                scatter(HALF - 1, 0)
                scatter(HALF - 1, 1)

            pool.memset(big1[:, 0:(NB + 1) * MW], 0.0).then_inc(s["sums_zero"], 1)
            pool.wait_ge(s["sums_zero"], 1)
            pool.wait_ge(s["items_ready"], 1)

            def buckets(i):
                return [pool.value_load(item_bkt[0:1, bass.ds(S3 * i + u, 1)], min_val=0, max_val=NB)
                        for u in range(S3)]

            def add_item(i, u, first, b):
                j = S3 * i + u
                pool.wait_ge(s["part_ready"], j + 1)
                if not first or u:
                    pool.wait_ge(s["part_added"], j)
                pool.sem_inc(s["pool_turn"], 1)
                dest = big1[:, bass.ds(b * MW, MW)]
                pool.tensor_tensor(dest, dest, part3[u % 2][:, :], ALU.add).then_inc(s["part_added"], 1)
            for u, b in enumerate(buckets(0)):
                add_item(0, u, True, b)
            with pool.Fori(1, ITEMS // S3) as i:
                for u, b in enumerate(buckets(i)):
                    add_item(i, u, False, b)

        @block.scalar
        def _(act):
            act.wait_ge(s["consts_ready"], 2)
            for u in range(2):
                act.dma_start(w1bd[u * R:(u + 1) * R, u * H:(u + 1) * H], w1t).then_inc(s["consts_in"], 16)
                act.dma_start(w2bd[u * H:(u + 1) * H, u * H:(u + 1) * H], w2t).then_inc(s["consts_in"], 16)
                act.dma_start(b1c[u * H:(u + 1) * H, :], b1).then_inc(s["consts_in"], 16)
                act.dma_start(w2bd[2 * H:2 * H + 1, u * H:(u + 1) * H], b2).then_inc(s["consts_in"], 16)
            act.dma_start(embt_s[:, :], embt).then_inc(s["consts_in"], 16)
            act.dma_start(adwt_s[:, :], adaptwt).then_inc(s["consts_in"], 16)
            act.dma_start(gam[:, :], gamma.partition_broadcast(P)).then_inc(s["gb_in"], 16)
            act.dma_start(bet[:, :], beta.partition_broadcast(P)).then_inc(s["gb_in"], 16)
            act.wait_ge(s["pt_psum"], 1)
            act.activation(pt_s[:, :], bank[1][0:GE, 0:NEL], ACT.Copy).then_inc(s["pt_ready"], 1)
            act.wait_ge(s["at_psum"], 1)
            act.activation(at_s[:, :], bank[1][0:NEL, 128:128 + NEL], ACT.Copy).then_inc(s["at_ready"], 1)
            act.wait_ge(s["dist_clip"], 1)
            act.activation(cutw[:, :], cutw[:, :], ACT.Sin, bias=half_pi[:, :],
                           scale=-math.pi / CUTOFF).then_inc(s["cos_ready"], 1)
            act.wait_ge(s["digits_ready"], 1)
            act.wait_ge(s["low_ready"], 1)
            with act.Fori(0, NB // ZB) as i:
                for k in range(ZB):
                    act.wait_ge(s["rows_psum"], ZB * i + k + 1)
                    act.activation(tb[:, bass.ds(i * ZB + k, 1), :, MW:TBL].rearrange("p b k c -> p (b k) c"),
                                   bank[1 + k][:, 0:3 * NEL].rearrange("p (k c) -> p k c", k=3),
                                   ACT.Copy).then_inc(s["rows_ready"], 1)

            def group(i, u, first):
                g = 2 * i + u
                prev, again = not first or u > 0, not first
                act.wait_ge(s["lot_psum"], g + 1)
                if prev:
                    act.wait_ge(s["place_psum"], g)
                act.activation(lot_s[:, :], oht_bank, ACT.Copy).then_inc(s["lot_ready"], 1)
                act.wait_ge(s["eat_psum"], g + 1)
                if prev:
                    act.wait_ge(s["hid_psum"], g)
                act.activation(eat_s[:, :], mlp_bank[0:2 * R, :], ACT.Copy).then_inc(s["eat_ready"], 1)
                act.wait_ge(s["loct_psum"], g + 1)
                if prev:
                    act.wait_ge(s["win_psum"], g)
                act.activation(loct_s[:, :], oht_bank, ACT.Copy).then_inc(s["loct_ready"], 1)
                act.wait_ge(s["hid_psum"], g + 1)
                if prev:
                    act.wait_ge(s["gate_psum"], g)
                act.activation(hid_s[0:2 * H, :], mlp_bank[0:2 * H, :], ACT.Silu,
                               bias=b1c[:, :]).then_inc(s["hid_ready"], 1)
                if again:
                    act.wait_ge(rec_out[u], P * i)
                act.activation(rec_t[u][:, :, H + 1], src_f[:, bass.ds(g * T, T)], ACT.Copy)\
                    .then_inc(s["side_ready"], 1)

            act.wait_ge(s["hilo_ready"], 1)
            group(0, 0, True)
            group(0, 1, True)
            with act.Fori(1, HALF) as i:
                group(i, 0, False)
                group(i, 1, False)

            def item(i, u, first):
                j = 2 * i + u
                act.wait_ge(s["part_psum"], j + 1)
                if not first:
                    act.wait_ge(s["part_added"], j - 1)
                act.activation(part3[u][:, :], bank[u][:, 0:MW], ACT.Copy).then_inc(s["part_ready"], 1)
            item(0, 0, True)
            item(0, 1, True)
            with act.Fori(1, ITEMS // 2) as i:
                item(i, 0, False)
                item(i, 1, False)
            for n in range(2):
                act.wait_ge(s["var_ready"], n + 1)
                act.activation(stat[1][:, :], stat[0][:, :], ACT.Sqrt).then_inc(s["std_ready"], 1)

        @block.vector
        def _(dve):
            step = [0]

            def link(ins):
                step[0] += 1
                ins.then_inc(s["dve_step"], 1)
                dve.wait_ge(s["dve_step"], step[0])

            dve.wait_ge(s["src_in"], 16)
            dig_a = src_f[:, :].bitcast(i32)
            link(nc.vector.tensor_scalar(dig_a, src_i[:, :], 10, None, ALU.logical_shift_right))
            link(nc.vector.tensor_scalar(hi_i[:, :], src_i[:, :], 7, NBL - 1,
                                         ALU.logical_shift_right, ALU.bitwise_and))
            dve.wait_ge(s["consts_ready"], 2)
            link(nc.vector.tensor_tensor(
                oh_a, dig_a.rearrange("p (g j) -> p g j", j=J).unsqueeze(2).to_broadcast([P, C // J, NA, J]),
                over_last(iota_f[:, 0:NA], J).unsqueeze(1).to_broadcast([P, C // J, NA, J]), ALU.is_equal))
            link(nc.vector.tensor_tensor(
                oh_b.rearrange("p g j b -> p (g j) b"), over_last(hi_i[:, :], NBL),
                over_mid(iota_f[:, 0:NBL], C), ALU.is_equal))
            nc.vector.tensor_copy(adapt[:, 0:1], iota_f[:, 0:1]).then_inc(s["hist_in"], 1)
            link(nc.vector.tensor_scalar(hi_i[:, :], src_i[:, :], 7, None, ALU.logical_shift_right))
            link(nc.vector.tensor_scalar(lo_i[:, :], src_i[:, :], P - 1, None, ALU.bitwise_and))
            nc.vector.tensor_copy(src_f[:, :], src_i[:, :]).then_inc(s["hilo_ready"], 1)
            dve.wait_ge(s["dist_in"], 16)
            nc.vector.tensor_scalar(cutw[:, :], dist[:, :], CUTOFF, None, ALU.min).then_inc(s["dist_clip"], 1)
            link(nc.vector.tensor_scalar(row_a[:, 0:1], row_i[:, :], 4, 3,
                                         ALU.logical_shift_right, ALU.logical_shift_left))
            link(nc.vector.tensor_scalar(row_a[:, 1:2], row_i[:, :], J - 1, None, ALU.bitwise_and))
            link(nc.vector.tensor_copy(row_af[:, :], row_a[:, :]))
            link(nc.vector.tensor_scalar(under_f[:, :, :], under_f[:, :, :], row_af[:, 0:1], None, ALU.is_gt))
            link(nc.vector.tensor_scalar(same_j[:, :], iota_f[:, 0:J], row_af[:, 1:2], None, ALU.is_equal))
            dve.wait_ge(s["dstg_in"], 16)
            link(nc.vector.tensor_reduce(low_g[:, :], dst_g, AX.X, ALU.min))
            link(nc.vector.tensor_reduce(high_g[:, :], dst_g, AX.X, ALU.max))
            link(nc.vector.tensor_scalar(low_g[:, :], low_g[:, :], float((NB - 1) * P), None, ALU.min))
            link(nc.vector.tensor_tensor(high_g[:, :], high_g[:, :], low_g[:, :], ALU.subtract))
            link(nc.vector.tensor_scalar(fits[:, :], high_g[:, :], float(P), None, ALU.is_lt))
            nc.vector.tensor_tensor(low_dg[:, :, :], over_last(low_g[:, :], GP), over_mid(ident_f[0:GP, 0:GP], GB),
                                    ALU.mult).then_inc(s["low_ready"], 1)
            dve.wait_ge(s["hist_ready"], 1)
            link(nc.vector.tensor_tensor(diag[:, :, :],
                                         bank[0][0:NA * J, 0:J * NBL].rearrange("p (j b) -> p j b", b=NBL),
                                         over_last(same_j[0:NA * J, :], NBL), ALU.mult))
            link(nc.vector.reduce_sum(digits[:, :], diag[:, :, :].rearrange("p j b -> p b j"), axis=AX.X))
            nc.vector.tensor_copy(adapt[:, 0:1], iota_f[:, 0:1]).then_inc(s["digits_ready"], 1)
            dve.wait_ge(s["base_psum"], 1)
            link(nc.vector.tensor_copy(base[:, :], bank[0][:, 256:256 + NB + 1]))
            link(nc.vector.tensor_copy(base_i[:, :], base[:, :]))

            dve.wait_ge(s["at_ready"], 1)
            link(nc.vector.tensor_copy(at3[:, 0, :], at_s[:, :]))
            link(nc.vector.tensor_tensor(at_r[:, :], at_s[:, :], at3[:, 0, :], ALU.subtract))
            link(nc.vector.tensor_copy(at3[:, 1, :], at_r[:, :]))
            link(nc.vector.tensor_tensor(at_r[:, :], at_r[:, :], at3[:, 1, :], ALU.subtract))
            nc.vector.tensor_copy(at3[:, 2, :], at_r[:, :]).then_inc(s["at3_ready"], 1)

            dve.wait_ge(s["zrow_in"], 16)
            dve.wait_ge(s["z_in"], 32)
            nc.vector.tensor_scalar(z_b[:, :], z_i[:, :], float(-ZBIAS), float(1 << ZSHIFT), ALU.add, ALU.mult)\
                .then_inc(s["zb_ready"], 1)

            def types(i, first):
                if not first:
                    dve.wait_ge(s["rows_psum"], ZB * i)
                nc.vector.tensor_scalar(zoh[:, :], zrow_i[:, bass.ds(i * (ZB * P), ZB * P)], iota_p[0:NEL, :],
                                        None, ALU.is_equal).then_inc(s["zoh_ready"], 1)
            types(0, True)
            with dve.Fori(1, NB // ZB) as i:
                types(i, False)
            dve.wait_ge(s["low_psum"], 1)
            link(nc.vector.tensor_copy(low_all[:, :], bank[0][:, 64:64 + G]))
            link(nc.vector.reduce_sum(fit_all[:, 0:1], bank[0][:, 0:GB], axis=AX.X))
            link(nc.vector.tensor_scalar(fit_all[:, 1:2], fit_all[:, 0:1], G - 0.5, None, ALU.is_gt))
            nc.vector.tensor_copy(low_i[:, :], low_all[0:1, :]).then_inc(s["windows_ready"], 1)
            nc.vector.tensor_copy(windowed[:, :], fit_all[0:1, 1:2]).then_inc(s["windows_ready"], 1)
            dve.wait_ge(s["cos_ready"], 1)
            link(nc.vector.tensor_scalar(cutw[:, :], cutw[:, :], 1.0, 0.5, ALU.add, ALU.mult))
            link(nc.vector.scalar_tensor_tensor(cutw[:, :], dist[:, :], CUTOFF, cutw[:, :],
                                                ALU.is_lt, ALU.mult))
            dve.wait_ge(s["dst_in"], 16)
            link(nc.vector.tensor_tensor(loc[:, :].rearrange("p (g t) -> p g t", t=T),
                                         dst_i[:, :].rearrange("p (g t) -> p g t", t=T),
                                         over_last(low_all[:, :], T), ALU.subtract))
            link(nc.vector.tensor_scalar(loc[:, :], loc[:, :], iota_p[:, :], fit_all[:, 1:2],
                                         ALU.subtract, ALU.mult))
            nc.vector.tensor_scalar(loc[:, :], loc[:, :], iota_p[:, :], None, ALU.add).then_inc(s["windows_ready"], 1)

            link(nc.vector.tensor_scalar(tmp_i[:, :], base_i[:, 0:NB], 9, None, ALU.arith_shift_right))
            link(nc.vector.tensor_scalar(first_c[:, :], tmp_i[:, :], float(CH - 1), None, ALU.min))
            link(nc.vector.tensor_scalar(tmp_f[:, :], base[:, 1:NB + 1], -1.0, None, ALU.add))
            link(nc.vector.tensor_copy(tmp_i[:, :], tmp_f[:, :]))
            link(nc.vector.tensor_scalar(tmp_i[:, :], tmp_i[:, :], 9, None, ALU.arith_shift_right))
            link(nc.vector.tensor_copy(tmp_f[:, :], tmp_i[:, :]))
            link(nc.vector.tensor_tensor(last_c[:, :], tmp_f[:, :], first_c[:, :], ALU.max))
            link(nc.vector.tensor_tensor(last_c[:, :], last_c[:, :], first_c[:, :], ALU.subtract))
            link(nc.vector.tensor_scalar(last_c[:, :], last_c[:, :], 1.0, None, ALU.add))
            link(nc.vector.tensor_tensor_scan(ends[:, :], ones_f[:, 0:NB], last_c[:, :], 0.0, ALU.mult, ALU.add))
            link(nc.vector.tensor_tensor(tmp_f[:, :], last_c[:, :], ends[:, :], ALU.subtract))
            link(nc.vector.tensor_tensor(first_c[:, :], first_c[:, :], tmp_f[:, :], ALU.add))
            link(nc.vector.memset(shift[:, :], 0.0))
            link(nc.vector.tensor_tensor(shift[:, 0:NB - 1], first_c[:, 1:NB], first_c[:, 0:NB - 1], ALU.subtract))
            link(nc.vector.tensor_tensor(past[:, :, :], over_mid(ends[:, :], IB), over_last(item_no[:, :], NB),
                                         ALU.is_le))
            link(nc.vector.tensor_tensor(past_d[:, :, :], past[:, :, :], over_mid(shift[:, 0:NB], IB), ALU.mult))
            link(nc.vector.reduce_sum(item_v[:, 0, :], past[:, :, :], axis=AX.X))
            link(nc.vector.reduce_sum(item_v[:, 1, :], past_d[:, :, :], axis=AX.X))
            link(nc.vector.tensor_tensor(item_v[:, 1, :], item_v[:, 1, :], item_no[:, :], ALU.add))
            link(nc.vector.tensor_scalar(item_v[:, 1, :], item_v[:, 1, :], float(CH - 1), None, ALU.min))
            for w in range(2):
                nc.vector.tensor_tensor(item_dg[:, w], over_last(item_v[0:IP, w, :], IP),
                                        over_mid(ident_f[0:IP, 0:IP], IB), ALU.mult).then_inc(s["items_diag"], 1)
            dve.wait_ge(s["item_psum"], 2)
            link(nc.vector.tensor_scalar(item_low[:, :], bank[6][:, 0:ITEMS], float(P), None, ALU.mult))
            nc.vector.tensor_copy(item_bkt[:, :], bank[6][0:1, 0:ITEMS]).then_inc(s["items_ready"], 1)
            nc.vector.tensor_copy(item_chk[:, :], bank[7][0:1, 0:ITEMS]).then_inc(s["items_ready"], 1)

            dve.wait_ge(s["windows_ready"], 3)

            def one_hots(g, prev):
                if prev:
                    dve.wait_ge(s["lot_psum"], g)
                nc.vector.tensor_tensor(oh_lo[:, :, :], over_last(lo_i[:, bass.ds(g * T, T)], P),
                                        over_mid(iota_f[:, :], T), ALU.is_equal).then_inc(s["lo_ready"], 1)
                if prev:
                    dve.wait_ge(s["place_psum"], g)
                nc.vector.tensor_tensor(oh_hi[:, :, :], over_last(hi_i[:, bass.ds(g * T, T)], NB),
                                        over_mid(iota_f[:, 0:NB], T), ALU.is_equal).then_inc(s["hi_ready"], 1)
                if prev:
                    dve.wait_ge(s["loct_psum"], g)
                nc.vector.tensor_tensor(oh_loc[:, :, :], over_last(loc[:, bass.ds(g * T, T)], P),
                                        over_mid(iota_f[:, :], T), ALU.is_equal).then_inc(s["loc_ready"], 1)

            def places(g, i, u, again):
                dve.wait_ge(s["hi_ready"], g + 1)
                dve.wait_ge(s["place_psum"], g + 1)
                nc.vector.tensor_tensor(picked[:, :, :], place_bank, oh_hi[:, :, :], ALU.mult)\
                    .then_inc(s["place_picked"], 1)
                nc.vector.tensor_tensor(base[:, 0:NB], base[:, 0:NB], count_bank, ALU.add)\
                    .then_inc(s["base_moved"], 1)
                dve.wait_ge(s["place_picked"], g + 1)
                nc.vector.reduce_sum(place_f[:, :], picked[:, :, :], axis=AX.X).then_inc(s["place_f_ready"], 1)
                dve.wait_ge(s["place_f_ready"], g + 1)
                nc.vector.tensor_copy(place_i[:, :], place_f[:, :]).then_inc(s["place_i_ready"], 1)
                dve.wait_ge(s["place_i_ready"], g + 1)
                nc.vector.tensor_scalar(z_edge[:, :], place_i[:, :], ZSHIFT, None, ALU.arith_shift_right)\
                    .then_inc(s["z_ready"], 1)
                if again:
                    dve.wait_ge(rec_out[u], P * i)
                nc.vector.tensor_scalar(pos_t[u][:, :].bitcast(i32), place_i[:, :], (1 << ZSHIFT) - 1, None,
                                        ALU.bitwise_and).then_inc(s["pos_ready"], 1)
                dve.wait_ge(s["z_ready"], g + 1)
                nc.vector.tensor_scalar(zs[:, :], z_edge[:, :], float(ZBIAS), None, ALU.add)\
                    .then_inc(s["zs_ready"], 1)

            def two(ap):
                return ap.rearrange("p (k t) c -> p k t c", t=2)

            def message(g, i, u, again):
                dve.wait_ge(s["win_psum"], g + 1)
                dve.wait_ge(s["zs_ready"], g + 1)
                for t in range(T):
                    nc.vector.scalar_tensor_tensor(junk[:, t, :], iota_f[:, 0:NEL], zs[:, t:t + 1],
                                                   win_bank[:, t // 2, t % 2, MW:TBL], ALU.is_equal, ALU.mult,
                                                   accum_out=adapt[:, t:t + 1]).then_inc(s["adapt_ready"], 1)
                if again:
                    dve.wait_ge(rec_out[u], P * i)
                nc.vector.tensor_copy(two(rec_t[u][:, :, H:MW]), win_bank[:, :, :, H:MW]).then_inc(s["wm_ready"], 1)
                dve.wait_ge(s["wm_ready"], 2 * g + 1)
                nc.vector.tensor_tensor(wm[:, :], rec_t[u][:, :, H], cutw[:, bass.ds(g * T, T)], ALU.mult)\
                    .then_inc(s["wm_ready"], 1)
                dve.wait_ge(s["gate_psum"], g + 1)
                dve.wait_ge(s["adapt_ready"], T * g + T)
                nc.vector.tensor_tensor(gate_s[:, :, :], gate_bank, over_last(adapt[:, :], H), ALU.add)\
                    .then_inc(s["gate_ready"], 1)
                dve.wait_ge(s["wm_ready"], 2 * g + 2)
                nc.vector.tensor_tensor(two(wh_s[:, :, :]), win_bank[:, :, :, 0:H],
                                        two(over_last(wm[:, :], H)), ALU.mult).then_inc(s["wh_ready"], 1)
                dve.wait_ge(s["gate_ready"], g + 1)
                dve.wait_ge(s["wh_ready"], g + 1)
                nc.vector.tensor_tensor(rec_t[u][:, :, 0:H], gate_s[:, :, :], wh_s[:, :, :], ALU.mult)\
                    .then_inc(s["rec_ready"], 1)

            one_hots(0, False)
            places(0, 0, 0, False)
            one_hots(1, True)
            message(0, 0, 0, False)
            places(1, 0, 1, False)
            one_hots(2, True)
            message(1, 0, 1, False)
            places(2, 1, 0, True)
            with dve.Fori(1, HALF - 1) as i:
                one_hots(2 * i + 1, True)
                message(2 * i, i, 0, True)
                places(2 * i + 1, i, 1, True)
                one_hots(2 * i + 2, True)
                message(2 * i + 1, i, 1, True)
                places(2 * i + 2, i + 1, 0, True)
            one_hots(G - 1, True)
            message(G - 2, HALF - 1, 0, True)
            places(G - 1, HALF - 1, 1, True)
            message(G - 1, HALF - 1, 1, True)

            def item(i, u, first):
                j = S3 * i + u
                v = u % 2
                dve.wait_ge(rec3_in[u], 16 * i + 16)
                if not first or u >= 2:
                    dve.wait_ge(s["part_psum"], j - 1)
                nc.vector.tensor_scalar(rel3[v][:, :], rec3[u][:, :, H + 1], item_low[:, bass.ds(j, 1)], None,
                                        ALU.subtract).then_inc(s["rel_ready"], 1)
                dve.wait_ge(s["rel_ready"], j + 1)
                nc.vector.tensor_tensor(oh3[v][:, :, :], over_mid(iota_f[:, :], K3), over_last(rel3[v][:, :], P),
                                        ALU.is_equal).then_inc(s["oh3_ready"], 1)
            for u in range(S3):
                item(0, u, True)
            with dve.Fori(1, ITEMS // S3) as i:
                for u in range(S3):
                    item(i, u, False)

            dve.wait_ge(s["part_added"], ITEMS)
            dve.wait_ge(s["xn_in"], 16)
            dve.wait_ge(s["gb_in"], 32)
            link(nc.vector.tensor_scalar(stat[0][:, :], sums[:, 0:NB, H], 1e-8, None, ALU.max))
            link(nc.vector.reciprocal(stat[1][:, :], stat[0][:, :]))
            link(nc.vector.tensor_tensor(y1, sums[:, 0:NB, 0:H], over_last(stat[1][:, :], H), ALU.mult))
            link(nc.vector.tensor_tensor(y1, y1, xn, ALU.add))

            def norm(y, n):
                link(nc.vector.reduce_sum(stat[0][:, :], y, axis=AX.X))
                link(nc.vector.tensor_scalar(stat[0][:, :], stat[0][:, :], 1.0 / H, None, ALU.mult))
                link(nc.vector.tensor_tensor(y, y, over_last(stat[0][:, :], H), ALU.subtract))
                link(nc.vector.tensor_tensor(sq, y, y, ALU.mult))
                link(nc.vector.reduce_sum(stat[0][:, :], sq, axis=AX.X))
                nc.vector.tensor_scalar(stat[0][:, :], stat[0][:, :], 1.0 / H, EPS, ALU.mult, ALU.add)\
                    .then_inc(s["var_ready"], 1)
                dve.wait_ge(s["std_ready"], n + 1)
                link(nc.vector.reciprocal(stat[0][:, :], stat[1][:, :]))
            norm(y1, 0)
            link(nc.vector.tensor_tensor(y1, y1, over_last(stat[0][:, :], H), ALU.mult))
            link(nc.vector.tensor_tensor(y1, y1, over_mid(gam[:, :], NB), ALU.mult))
            link(nc.vector.tensor_tensor(y1, y1, over_mid(bet[:, :], NB), ALU.add))
            link(nc.vector.tensor_tensor(y1, y1, xn, ALU.add))
            norm(y1, 1)
            nc.vector.tensor_tensor(y2, y1, over_last(stat[0][:, :], H), ALU.mult).then_inc(s["y_ready"], 1)

        @block.tensor
        def _(pe):
            pe.wait_ge(s["consts_in"], 16 * 10)
            nc.tensor.matmul(bank[1][0:GE, 0:NEL], adwt_s[:, :], embt_s[:, :], start=True, stop=True)\
                .then_inc(s["pt_psum"], 1)
            pe.wait_ge(s["pt_ready"], 1)
            nc.tensor.matmul(bank[1][0:NEL, 128:128 + NEL], pt_s[:, :], embt_s[:, :], start=True, stop=True)\
                .then_inc(s["at_psum"], 1)
            pe.wait_ge(s["hist_in"], 1)
            hist = bank[0][0:NA * J, 0:J * NBL]

            def count(c, start, stop):
                return nc.tensor.matmul(hist, oh_a[:, c, :, :].rearrange("p a j -> p (a j)"),
                                        oh_b[:, c, :, :].rearrange("p j b -> p (j b)"), start=start, stop=stop)
            for c in range(C // J):
                last = count(c, c == 0, c == C // J - 1)
            last.then_inc(s["hist_ready"], 1)
            pe.wait_ge(s["digits_ready"], 1)
            for b in range(NBL):
                last = nc.tensor.matmul(bank[0][:, 256:256 + NB + 1],
                                        digits[:, b:b + 1].to_broadcast([NA * J, P]), under_f[0:NA * J, b, :],
                                        start=b == 0, stop=b == NBL - 1)
            last.then_inc(s["base_psum"], 1)
            pe.wait_ge(s["low_ready"], 1)
            pe.wait_ge(s["zb_ready"], 1)
            nc.tensor.matmul(bank[0][:, 0:GB], ones_f[0:GP, :], fits[:, :], start=True, stop=True)
            nc.tensor.matmul(bank[0][:, 64:64 + G], ones_f[0:GP, :], low_dg[:, :, :], start=True, stop=True)\
                .then_inc(s["low_psum"], 1)
            pe.wait_ge(s["at3_ready"], 1)

            def types(i, first):
                pe.wait_ge(s["zoh_ready"], i + 1)
                for k in range(ZB):
                    if not first:
                        pe.wait_ge(s["rows_ready"], ZB * i + k - ZB + 1)
                    nc.tensor.matmul(bank[1 + k][:, 0:3 * NEL], zoh[:, k * P:(k + 1) * P],
                                     at3[:, :, :].rearrange("z k c -> z (k c)"), start=True, stop=True)\
                        .then_inc(s["rows_psum"], 1)
            types(0, True)
            with pe.Fori(1, NB // ZB) as i:
                types(i, False)
            pe.wait_ge(s["rows_ready"], NB)
            for w in range(2):
                pe.wait_ge(s["items_diag"], w + 1)
                nc.tensor.matmul(bank[6 + w][:, 0:ITEMS], ones_f[0:IP, :],
                                 item_dg[:, w].rearrange("p b c -> p (b c)"), start=True, stop=True)\
                    .then_inc(s["item_psum"], 1)
            pe.wait_ge(s["items_ready"], 2)
            pe.wait_ge(s["windows_ready"], 3)

            def group(i, u, first, windowed):
                g = 2 * i + u
                prev = not first or u > 0
                pe.wait_ge(s["lo_ready"], g + 1)
                if prev:
                    pe.wait_ge(s["loct_ready"], g)
                for t in range(T):
                    last = nc.tensor.transpose(oht_bank[:, t * P:(t + 1) * P], oh_lo[:, t, :], ident_b[:, :])
                last.then_inc(s["lot_psum"], 1)
                pe.wait_ge(ea_in[u], 16 * i + 16)
                if prev:
                    pe.wait_ge(s["hid_ready"], g)
                for k in range(T // 2):
                    last = nc.tensor.transpose(mlp_bank[0:2 * R, k * P:(k + 1) * P],
                                               ea_t[u][:, 2 * R * k:2 * R * (k + 1)], ident_f[:, :])
                last.then_inc(s["eat_psum"], 1)
                pe.wait_ge(s["hi_ready"], g + 1)
                if prev:
                    pe.wait_ge(s["base_moved"], g)
                nc.tensor.matmul(place_bank, ident_f[:, :], over_mid(base[:, 0:NB], T), start=True, stop=False,
                                 skip_group_check=True)
                nc.tensor.matmul(place_bank, before_b[:, :], oh_hi[:, :, :], start=False, stop=False,
                                 skip_group_check=True)
                for t in range(T - 1):
                    nc.tensor.matmul(place_bank[:, t + 1:T, :], ones_b[:, :],
                                     over_mid(oh_hi[:, t, :], T - 1 - t), start=False, stop=False,
                                     skip_group_check=True)
                pe.wait_ge(s["lot_ready"], g + 1)
                for t in range(T):
                    nc.tensor.matmul(place_bank[:, t, :], lot_s[:, t * P:(t + 1) * P], z_b[:, :],
                                     start=False, stop=True, skip_group_check=True)
                for t in range(T):
                    last = nc.tensor.matmul(count_bank, ones_b[:, :], oh_hi[:, t, :],
                                            start=t == 0, stop=t == T - 1)
                last.then_inc(s["place_psum"], 1)
                pe.wait_ge(s["loc_ready"], g + 1)
                for t in range(T):
                    last = nc.tensor.transpose(oht_bank[:, t * P:(t + 1) * P], oh_loc[:, t, :], ident_b[:, :])
                last.then_inc(s["loct_psum"], 1)
                pe.wait_ge(s["eat_ready"], g + 1)
                nc.tensor.matmul(mlp_bank[0:2 * H, :], w1bd[:, :], eat_s[:, :], start=True, stop=True)\
                    .then_inc(s["hid_psum"], 1)
                pe.wait_ge(s["loct_ready"], g + 1)
                if windowed:
                    pe.wait_ge(win_in[u], 16 * i + 16)
                else:
                    pe.wait_ge(rows_in[u], P * i + P)
                if prev:
                    pe.wait_ge(s["wh_ready"], g)
                for t in range(T):
                    for k in range(3):
                        last = nc.tensor.matmul(win_bank[:, t // 2, t % 2, :], loct_s[:, t * P:(t + 1) * P],
                                                win_t[u][:, 0 if windowed else t, k * TBL:(k + 1) * TBL],
                                                start=k == 0, stop=k == 2)
                last.then_inc(s["win_psum"], 1)
                pe.wait_ge(s["hid_ready"], g + 1)
                if prev:
                    pe.wait_ge(s["gate_ready"], g)
                for k in range(T // 2):
                    last = nc.tensor.matmul(gate_psum[:, 2 * H * k:2 * H * (k + 1)], hid_s[:, k * P:(k + 1) * P],
                                            w2bd[:, :], start=True, stop=True)
                last.then_inc(s["gate_psum"], 1)

            def groups(windowed):
                group(0, 0, True, windowed)
                group(0, 1, True, windowed)
                with pe.Fori(1, HALF) as i:
                    group(i, 0, False, windowed)
                    group(i, 1, False, windowed)
            fast = pe.value_load(windowed[0:1, 0:1], min_val=0, max_val=1)
            with pe.If(fast > 0):
                groups(True)
            with pe.Else():
                groups(False)

            def item(i, u, first):
                j = S3 * i + u
                v = u % 2
                pe.wait_ge(s["oh3_ready"], j + 1)
                if not first or u >= 2:
                    pe.wait_ge(s["part_ready"], j - 1)
                for t in range(K3):
                    last = nc.tensor.matmul(bank[v][:, 0:MW], oh3[v][:, t, :], rec3[u][:, t, 0:MW],
                                            start=t == 0, stop=t == K3 - 1)
                last.then_inc(s["part_psum"], 1)
            for u in range(S3):
                item(0, u, True)
            with pe.Fori(1, ITEMS // S3) as i:
                for u in range(S3):
                    item(i, u, False)


def kernel(x, src, dst, edge_attr_40, edge_weight, node_type_119, node_vec, L0_gnn_W1, L0_gnn_b1,
           L0_gnn_W2, L0_gnn_b2, L0_gnn_emb, L0_gnn_adaptW, L0_gnn_gamma, L0_gnn_beta):
    import numpy as np
    import concourse.bacc as bacc
    from concourse.bass_utils import run_bass_kernel_spmd as run

    nc = bacc.Bacc("TRN2", target_bir_lowering=False, num_devices=1)
    pad = EP - E
    npad = NB * P - N

    def edges(a, fill):
        a = np.concatenate([np.asarray(a), np.full((pad,), fill, a.dtype)])
        return np.ascontiguousarray(a.reshape(G, P, T).transpose(1, 0, 2).reshape(P, C))

    def nodes(a):
        return np.ascontiguousarray(np.concatenate([np.asarray(a), np.zeros((npad,), a.dtype)]))

    arrays = {
        "in_x": np.concatenate([np.asarray(x), np.zeros((npad, H), np.float32)]),
        "in_src": edges(src, NB * P - 1),
        "in_dst_edges": edges(dst, N - 1),
        "in_dst": np.concatenate([np.asarray(dst), np.full((pad,), N - 1, np.int32)]).reshape(G * P, T),
        "in_weight": edges(edge_weight, 0),
        "in_ea": np.concatenate([np.asarray(edge_attr_40), np.zeros((pad, R), np.float32)]).reshape(G * P, T * R),
        "in_z_nodes": np.ascontiguousarray(nodes(node_type_119).reshape(NB, P).T),
        "in_z_row": nodes(node_type_119),
        "in_mult": np.ascontiguousarray(nodes(node_vec).reshape(NB, P).T),
        "in_w1t": np.ascontiguousarray(np.asarray(L0_gnn_W1).T),
        "in_b1": np.asarray(L0_gnn_b1).reshape(H, 1),
        "in_w2t": np.ascontiguousarray(np.asarray(L0_gnn_W2).T),
        "in_b2": np.asarray(L0_gnn_b2).reshape(1, H),
        "in_embt": np.ascontiguousarray(np.asarray(L0_gnn_emb).T),
        "in_adaptwt": np.ascontiguousarray(np.asarray(L0_gnn_adaptW).T),
        "in_gamma": np.asarray(L0_gnn_gamma),
        "in_beta": np.asarray(L0_gnn_beta),
    }
    args = []
    for name, a in arrays.items():
        dt = mybir.dt.from_np(a.dtype)
        if name == "in_dst":
            dt = mybir.dt.uint32
            arrays[name] = a.view(np.uint32)
        args.append(nc.dram_tensor(name, a.shape, dt, kind="ExternalInput").ap())
    args.append(nc.dram_tensor("node_table", (NB * P, 3 * TBL), mybir.dt.bfloat16, kind="Internal").ap())
    args.append(nc.dram_tensor("sorted_rec", (EP, REC), mybir.dt.float32, kind="Internal").ap())
    args.append(nc.dram_tensor("out", (N, H), mybir.dt.float32, kind="ExternalOutput").ap())
    build(nc, *args)
    return run(nc, [arrays], core_ids=[0]).results[0]["out"]
```

```python
import math
from contextlib import ExitStack

import concourse.bass as bass
from concourse import mybir


N, H, R, NEL, GE = 6250, 48, 40, 119, 32
E = 206250
P = 128
NB = -(-N // P)
T = 8
G = -(-E // (P * T))
EP = G * P * T
C = G * T
TBL = H + 1 + NEL
MW = H + 1
PW = 3 * MW
REC = (PW + 1) // 2 + 1
NA, NBL = 7, 8
J = 16
ZB = 7
ZL = 4
K3 = 8
CH = EP // (P * K3)
CSHIFT = (P * K3).bit_length() - 1
PA = 37
GA = 2 * PA
STARTS = (0, GA, G)
EARLY = G - GA - 2
assert K3 == T and EARLY >= GA + NB
IB = 4
IP = -(-(G - GA + NB) // IB)
GB, GP = 2, G // 2
ZSHIFT, ZBIAS = 18, 64
ITEMS = IB * IP
assert EARLY <= ITEMS
S3 = 6
CUTOFF = 6.0
EPS = 1e-5


def build(nc, x, src, src_rows, dst_rows, weight, ea, z_nodes, z_row, mult_nodes,
          w1t, b1, w2t, b2, embt, adaptwt, gamma, beta, table, node_rows, sorted_rec, out):
    f32, bf16 = mybir.dt.float32, mybir.dt.bfloat16
    i32, u32 = mybir.dt.int32, mybir.dt.uint32
    ALU, ACT, AX = mybir.AluOpType, mybir.ActivationFunctionType, mybir.AxisListType
    ctx = ExitStack()
    with ctx:
        def sb(name, shape, dt):
            return ctx.enter_context(nc.sbuf_tensor(name, shape, dt))

        def sem(name):
            return ctx.enter_context(nc.semaphore(name))

        bank4 = ctx.enter_context(nc.psum_tensor("banks0_3", [P, 4 * 512], f32))
        bank = [bank4[:, 512 * i:512 * (i + 1)] for i in range(4)] +\
            [ctx.enter_context(nc.psum_tensor(f"bank{i}", [P, 512], f32)) for i in range(4, 8)]

        src_i = sb("src_i", [P, C], i32)
        hi_i = sb("hi_i", [P, C], i32)
        src_f = sb("src_f", [P, C], f32)
        dist = sb("dist", [P, C], f32)
        rows_b = sb("rows_b", [GP, GB, 2, P * T], bf16)
        cutw = sb("cutw", [P, C], f32)
        big1 = sb("big1", [P, NB * 3 * TBL // 2], f32)
        big2 = sb("big2", [P, 6464], f32)
        tb = big1[:, :].bitcast(bf16).rearrange("p (b k c) -> p b k c", k=3, c=TBL)
        iota_f = sb("iota_f", [P, P], f32)
        iota_p = sb("iota_p", [P, 1], f32)
        ident_f = sb("ident_f", [P, P], f32)
        before_b = sb("before_b", [P, P], bf16)
        ones_b = sb("ones_b", [P, P], bf16)
        ones_f = sb("ones_f", [P, P], f32)
        row_i = sb("row_i", [P, 1], i32)
        row_a = sb("row_a", [P, 2], i32)
        row_af = sb("row_af", [P, 2], f32)
        under_f = sb("under_f", [P, NBL, NB + 1], f32)
        same_j = sb("same_j", [P, J], f32)
        diag = sb("diag", [NA * J, 2, NBL, J], f32)
        w1bd = sb("w1bd", [2 * R, 2 * H], f32)
        w2bd = sb("w2bd", [2 * H + 1, 2 * H], f32)
        b1c = sb("b1c", [2 * H, 1], f32)
        embt_s = sb("embt_s", [GE, NEL], f32)
        adwt_s = sb("adwt_s", [GE, GE], f32)
        pt_s = sb("pt_s", [GE, NEL], f32)
        at_s = sb("at_s", [NEL, NEL], f32)
        z_i = sb("z_i", [P, NB], i32)
        z_b = sb("z_b", [P, NB], bf16)
        at_r = sb("at_r", [NEL, NEL], f32)
        at3 = sb("at3", [NEL, 3, NEL], bf16)
        low_g = sb("low_g", [GP, GB], f32)
        high_g = sb("high_g", [GP, GB], f32)
        fits = sb("fits", [GP, GB], f32)
        low_dg = sb("low_dg", [GP, GB, GP], f32)
        fit_all = sb("fit_all", [P, 2], f32)
        low_i = sb("low_i", [1, G], i32)
        windowed = sb("windowed", [1, 1], i32)
        mult_s = sb("mult_s", [P, NB], f32)
        digits = sb("digits", [NA * J, 2, NBL], f32)
        starts = sb("starts", [P, 2, NB + 1], f32)
        base = sb("base", [P, NB], f32)
        half_pi = sb("half_pi", [P, 1], f32)
        starts_i = sb("starts_i", [P, 2, NB + 1], i32)
        first_c = sb("first_c", [P, NB], f32)
        last_c = sb("last_c", [P, NB], f32)
        chunk_i = sb("chunk_i", [P, NB], i32)
        chunk_f = sb("chunk_f", [P, NB], f32)
        ends = sb("ends", [P, NB], f32)
        shift = sb("shift", [P, NB + 1], f32)
        item_no = sb("item_no", [P, IB], f32)
        past = sb("past", [P, IB, NB], f32)
        past_d = sb("past_d", [P, IB, NB], f32)
        item_v = sb("item_v", [P, 2, IB], f32)
        item_dg = sb("item_dg", [IP, 2, 2, IB, IP], f32)
        item_low = sb("item_low", [P, 2 * ITEMS], f32)
        item_bkt = sb("item_bkt", [1, 2 * ITEMS], i32)
        item_chk = sb("item_chk", [1, 2 * ITEMS], i32)

        ea_t = [sb(f"ea_t{u}", [P, T * R], f32) for u in range(2)]
        dst_t = [sb(f"dst_t{u}", [P, T], u32) for u in range(2)]
        rec_t = [sb(f"rec_t{u}", [P, T, REC], f32) for u in range(2)]
        pos_t = [sb(f"pos_t{u}", [P, T], u32) for u in range(2)]
        eat_s = sb("eat_s", [2 * R, 512], f32)
        hid_s = sb("hid_s", [2 * H + 1, 512], f32)
        oh_hi = [sb(f"oh_hi{u}", [P, T, NB], bf16) for u in range(2)]
        picked = sb("picked", [P, T, NB], f32)
        place_f = sb("place_f", [P, T], f32)
        place_i = sb("place_i", [P, T], i32)
        z_edge = sb("z_edge", [P, T], i32)
        zs = sb("zs", [P, T], f32)
        adapt = sb("adapt", [P, T], f32)
        junk = big2[:, 0:T * NEL].rearrange("p (t c) -> p t c", c=NEL)
        wm = sb("wm", [P, T], f32)
        gate_s = sb("gate_s", [P, T, H], f32)
        wh_s = sb("wh_s", [P, T, H], f32)
        msg_s = sb("msg_s", [P, T, MW], f32)
        msg_r = sb("msg_r", [P, T, MW], f32)

        rec3_all = sb("rec3_all", [P, S3 * K3 * REC], f32)
        rec3 = [rec3_all[:, u * K3 * REC:(u + 1) * K3 * REC].rearrange("p (t c) -> p t c", c=REC)
                for u in range(S3)]
        oh3_all = sb("oh3_all", [P, 2 * K3 * P], f32)
        oh3 = [oh3_all[:, u * K3 * P:(u + 1) * K3 * P].bitcast(bf16)[:, 0:K3 * P]
               .rearrange("p (t c) -> p t c", c=P) for u in range(2)]
        loc_g = oh3_all[0:GP, 0:GB * P * T].rearrange("p (b e) -> p b e", b=GB)
        apart = oh3_all[:, K3 * P // 2:K3 * P].bitcast(bf16).rearrange("p (t c) -> p t c", c=P)
        rel = sb("rel", [P, K3], f32)
        part3 = [sb(f"part3_{u}", [P, PW], f32) for u in range(2)]
        gam = sb("gam", [P, H], f32)
        bet = sb("bet", [P, H], f32)
        stat = [sb(f"stat{i}", [P, NB], f32) for i in range(2)]

        oh_a = big1[:, 0:C * NA // 2].bitcast(bf16).rearrange("p (g a j) -> p g a j", a=NA, j=J)
        oh_b = big2[:, 0:C * NBL // 2].bitcast(bf16).rearrange("p (b c) -> p b c", b=NBL)
        dig_a, dig_b = (cutw[:, o:o + C // 2].bitcast(bf16) for o in (0, C // 2))
        work = sb("work", [P, NB * P], f32)
        zrow_i = work[0:NEL, :].bitcast(i32)
        WW, WO = T * 3 * TBL // 2, T * P // 2
        win_t = [work[:, u * WW:(u + 1) * WW].bitcast(bf16).rearrange("p (t c) -> p t c", t=T) for u in range(2)]
        oht = [work[:, 2 * WW + 2 * u * WO:2 * WW + 2 * (u + 1) * WO].bitcast(bf16)
               .rearrange("p (k e) -> p k e", k=2) for u in range(2)]
        dst_g, src_g = (big1[0:GP, 8192 + o:8192 + o + GB * P * T].bitcast(i32)
                        .rearrange("p (b e) -> p b e", b=GB) for o in (0, GB * P * T))
        row_t = [a[:, 0:P * T].bitcast(bf16) for a in (src_i, dist)]
        zoh = big2[0:NEL, 0:NB * P // 2].bitcast(bf16)
        own_row = rec3_all[0:GP, 2560:2560 + P * T]
        xm = rec3_all[:, 0:NB * MW].rearrange("p (b c) -> p b c", c=MW)
        SW = (NB + 1) * PW
        sums = big1[:, 0:SW].rearrange("p (b k c) -> p b k c", k=3, c=MW)
        xn = big1[:, SW:SW + NB * H].rearrange("p (b c) -> p b c", c=H)
        y1 = big1[:, SW + NB * H:SW + 2 * NB * H].rearrange("p (b c) -> p b c", c=H)
        rec_b = [a[:, :, :].bitcast(bf16)[:, :, 0:PW].rearrange("p t (k c) -> p t k c", k=3) for a in rec_t]
        xb = work[:, 0:NB * H].rearrange("p (b c) -> p b c", c=H)
        y2 = big2[:, 0:NB * H].rearrange("p (b c) -> p b c", c=H)
        sq = big2[:, 2560:2560 + NB * H].rearrange("p (b c) -> p b c", c=H)

        names = """src_in dist_in consts_in z_in zrow_in x_in dstg_in srcg_in table_out row_table_out rows_b_ready
            pool_turn dve_turn pool_step consts_ready dve_step hist_in hist_ready digits_ready base_psum base_read
            pt_psum pt_ready at_psum at_ready at3_ready zoh_ready rows_psum rows_ready split_ready left_x_ready
            zb_ready dist_clip cos_ready cutw_ready hilo_ready low_ready low_psum windows_ready
            hi_ready oht_ready place_psum place_picked place_f_ready place_i_ready pos_ready
            z_ready zs_ready base_moved eat_psum eat_ready
            hid_psum hid_ready gate_psum gate_ready win_psum adapt_ready wm_ready wh_ready
            msg_ready part0_ready left_ready part1_ready rec_ready side_ready items_diag item_psum items_ready
            oh3_ready part_psum part_ready part_added sums_zero xn_in gb_in
            rel_ready apart_ready early_oh_ready early_psum early_added
            centred_ready sq_ready var_ready std_ready y_ready out_done""".split()
        s = {n: sem(n) for n in names}
        ea_in = [sem(f"ea_in{u}") for u in range(2)]
        idx_in = [sem(f"idx_in{u}") for u in range(2)]
        win_in = [sem(f"win_in{u}") for u in range(2)]
        row_in = [sem(f"row_in{u}") for u in range(2)]
        rows_in = [sem(f"rows_in{u}") for u in range(2)]
        rec_out = [sem(f"rec_out{u}") for u in range(2)]
        early_in = [sem(f"early_in{u}") for u in range(2)]
        rec3_in = [sem(f"rec3_in{u}") for u in range(S3)]
        block = ctx.enter_context(nc.Block())

        def over_last(ap, n):
            return ap.unsqueeze(ap.ndim).to_broadcast(list(ap.shape) + [n])

        def over_mid(ap, n):
            return ap.unsqueeze(1).to_broadcast([ap.shape[0], n] + list(ap.shape[1:]))

        win_bank = bank4[:, :].rearrange("p (k c) -> p k c", k=T // 2)[:, :, 0:2 * TBL]\
            .rearrange("p k (t c) -> p k t c", t=2)
        mlp_bank, gate_psum, place_psum = bank[4], bank[5], bank[7]
        hist = [bank[0][0:NA * J, J * NBL * h:J * NBL * (h + 1)] for h in range(2)]
        gate_bank = gate_psum[:, 0:T * H].rearrange("p (t c) -> p t c", c=H)
        place_bank = place_psum[:, 0:T * NB].rearrange("p (t c) -> p t c", c=NB)
        count_bank = place_psum[:, T * NB:(T + 1) * NB]
        HALF = G // 2

        def chunk_of(eng, j):
            return eng.value_load(item_chk[0:1, bass.ds(j, 1)], min_val=0, max_val=CH - 1)

        def load_chunk(eng, u, c, signal=None):
            eng.dma_start(rec3[u][:, :, :], sorted_rec[bass.ds(c * (P * K3), P * K3), :]
                          .rearrange("(p t) c -> p t c", t=K3)).then_inc(signal or rec3_in[u], 16)

        HALVES = ((0, ZL * ZB), (ZL * ZB, NB))

        @block.sync
        def _(sp):
            sp.dma_start(src_i[:, :], src).then_inc(s["src_in"], 16)
            sp.dma_start(dst_g, dst_rows.rearrange("(g b p) t -> g b (p t)", b=GB, p=P).bitcast(i32))\
                .then_inc(s["dstg_in"], 16)
            sp.dma_start(z_i[:, :], z_nodes).then_inc(s["z_in"], 16)
            sp.dma_start(mult_s[:, :], mult_nodes).then_inc(s["z_in"], 16)
            sp.dma_start(dist[:, :], weight).then_inc(s["dist_in"], 16)
            sp.dma_start(zrow_i, z_row.partition_broadcast(NEL)).then_inc(s["zrow_in"], 16)
            sp.wait_ge(s["consts_in"], 16 * 10)
            sp.dma_start(xm[:, :, 0:H], x.rearrange("(b p) c -> p b c", p=P)).then_inc(s["x_in"], 16)
            sp.dma_start(src_g, src_rows.rearrange("(g b p) t -> g b (p t)", b=GB, p=P))\
                .then_inc(s["srcg_in"], 16)
            sp.wait_ge(s["rows_b_ready"], GB)
            sp.dma_start(node_rows.rearrange("(g b) e -> g (b e)", b=GB),
                         rows_b[:, :, :, :].rearrange("g b k e -> g (b k e)")).then_inc(s["row_table_out"], 16)
            def attributes(i, u, first):
                g = 2 * i + u
                if not first:
                    sp.wait_ge(s["eat_psum"], g - 1)
                sp.dma_start(ea_t[u][:, :], ea[bass.ds(g * P, P), :]).then_inc(ea_in[u], 16)
                if not first:
                    sp.wait_ge(s["oht_ready"], g - 1)
                sp.dma_start(row_t[u], node_rows[bass.ds(g, 1), :].rearrange("a e -> (a e)")
                             .partition_broadcast(P)).then_inc(row_in[u], 16)

            def table_part(h):
                first_b, end = HALVES[h]
                sp.wait_ge(s["rows_ready"], end)
                sp.wait_ge(s["split_ready"], 3 * h + 3)
                sp.dma_start(table[first_b * P:end * P, :].rearrange("(b p) c -> p b c", p=P),
                             tb[:, first_b:end].rearrange("p b k c -> p b (k c)")).then_inc(s["table_out"], 16)
            table_part(0)
            sp.wait_ge(s["row_table_out"], 16)
            sp.wait_ge(s["cutw_ready"], 1)
            for u in range(2):
                attributes(0, u, True)
            table_part(1)

            def window(i, u, first, low):
                g = 2 * i + u
                if low is not None:
                    if not first:
                        sp.wait_ge(s["win_psum"], g - 1)
                    sp.dma_start(win_t[u][:, 0, :], table[bass.ds(low, P), :]).then_inc(win_in[u], 16)
                else:
                    if not first:
                        sp.wait_ge(rows_in[u], 16 * T * i)
                    sp.dma_start(dst_t[u][:, :], dst_rows[bass.ds(g * P, P), :]).then_inc(idx_in[u], 16)

            def lows(i):
                return [sp.value_load(low_i[0:1, bass.ds(i + u * GP, 1)], min_val=0, max_val=(NB - 1) * P)
                        for u in range(2)]

            sp.wait_ge(s["items_ready"], 2)
            sp.wait_ge(s["windows_ready"], 2)
            fast = sp.value_load(windowed[0:1, 0:1], min_val=0, max_val=1)
            sp.wait_ge(s["table_out"], 32)
            def early_chunk(m, u, first):
                c = chunk_of(sp, m)
                if first:
                    for v in range(2):
                        sp.wait_ge(rec_out[v], 16 * T * PA)
                else:
                    sp.wait_ge(s["early_psum"], m - 1)
                load_chunk(sp, u, c, early_in[u])

            def group(i, u, low, m=None, first=False):
                attributes(i, u, False)
                if m is not None:
                    early_chunk(m, 1 - u, first)
                window(i, u, False, low)

            def groups(low_of):
                for u, low in enumerate(low_of(0)):
                    window(0, u, True, low)
                with sp.Fori(1, PA + 1) as i:
                    for u, low in enumerate(low_of(i)):
                        group(i, u, low)
                low = low_of(PA + 1)
                group(PA + 1, 0, low[0])
                group(PA + 1, 1, low[1], 0, True)
                low = low_of(PA + 2)
                group(PA + 2, 0, low[0], 1, True)
                group(PA + 2, 1, low[1], 2)
                with sp.Fori(PA + 3, HALF) as i:
                    for u, low in enumerate(low_of(i)):
                        group(i, u, low, 2 * i + u - (GA + 3))
            with sp.If(fast > 0):
                groups(lows)
            with sp.Else():
                groups(lambda i: (None, None))
            early_chunk(EARLY - 1, 1, False)

            sp.dma_start(xn, x.rearrange("(b p) c -> p b c", p=P)).then_inc(s["xn_in"], 16)
            first_chunks = [chunk_of(sp, ITEMS + u) for u in range(S3)]
            sp.wait_ge(s["early_psum"], EARLY)
            for u in range(2):
                sp.wait_ge(rec_out[u], 16 * T * HALF)
            for u, c in enumerate(first_chunks):
                load_chunk(sp, u, c)
            with sp.Fori(1, ITEMS // S3) as i:
                for u, c in [(u, chunk_of(sp, ITEMS + S3 * i + u)) for u in range(0, S3, 2)]:
                    sp.wait_ge(s["part_psum"], S3 * i + u - S3 + 1)
                    load_chunk(sp, u, c)

            sp.wait_ge(s["y_ready"], 1)
            full = N // P
            end = HALVES[0][1]
            sp.dma_start(out[0:end * P, :].rearrange("(b p) c -> p b c", p=P),
                         y2[:, 0:end, :]).then_inc(s["out_done"], 16)
            sp.wait_ge(s["y_ready"], 2)
            sp.dma_start(out[end * P:full * P, :].rearrange("(b p) c -> p b c", p=P),
                         y2[:, end:full, :]).then_inc(s["out_done"], 16)
            sp.dma_start(out[full * P:N, :], y2[0:N - full * P, full, :]).then_inc(s["out_done"], 16)
            sp.wait_ge(s["out_done"], 48)

        @block.gpsimd
        def _(pool):
            step = [0]

            def link(ins):
                step[0] += 1
                ins.then_inc(s["pool_step"], 1)
                pool.wait_ge(s["pool_step"], step[0])

            def iota(t, pattern, cm):
                link(pool.iota(t, pattern, base=0, channel_multiplier=cm, allow_small_or_imprecise_dtypes=True))

            iota(iota_f[:, :], [[1, P]], 0)
            iota(iota_p[:, :], [[0, 1]], 1)
            iota(row_i[:, :], [[0, 1]], 1)
            iota(under_f[:, :, :], [[-1, NBL], [1, NB + 1]], 0)
            iota(item_no[:, :], [[IP, IB]], 1)
            iota(own_row, [[1, P], [0, T]], 0)
            link(pool.memset(ones_b[:, :], 1.0))
            link(pool.memset(ones_f[:, :], 1.0))
            for u in range(2):
                link(pool.memset(rec_t[u][:, :, :], 0.0))
            link(pool.memset(hid_s[2 * H:2 * H + 1, :], 1.0))
            link(pool.memset(half_pi[:, :], math.pi / 2))
            link(pool.memset(ident_f[:, :], 0.0))
            link(pool.memset(before_b[:, :], 1.0))
            link(pool.affine_select(out=ident_f[:, :], in_=ident_f[:, :], compare_op=ALU.not_equal, fill=1.0,
                                    base=0, pattern=[[-1, P]], channel_multiplier=1))
            link(pool.affine_select(out=before_b[:, :], in_=before_b[:, :], compare_op=ALU.is_gt, fill=0.0,
                                    base=0, pattern=[[1, P]], channel_multiplier=-1))
            pool.memset(w1bd[:, :], 0.0).then_inc(s["consts_ready"], 1)
            pool.memset(w2bd[:, :], 0.0).then_inc(s["consts_ready"], 1)

            def gather(i, u):
                pool.wait_ge(idx_in[u], 16 * i + 16)
                pool.sem_inc(s["pool_turn"], 1)
                for t in range(T):
                    pool.indirect_dma_start(win_t[u][:, t, :], None, table,
                                            bass.IndirectOffsetOnAxis(ap=dst_t[u][:, t:t + 1], axis=0))\
                        .then_inc(rows_in[u], 16)

            def scatter(i, u):
                g = 2 * i + u
                pool.wait_ge(s["rec_ready"], g + 1)
                pool.wait_ge(s["side_ready"], g + 1)
                pool.wait_ge(s["pos_ready"], g + 1)
                pool.sem_inc(s["pool_turn"], 1)
                for t in range(T):
                    pool.indirect_dma_start(sorted_rec, bass.IndirectOffsetOnAxis(ap=pos_t[u][:, t:t + 1], axis=0),
                                            rec_t[u][:, t, :], None).then_inc(rec_out[u], 16)

            pool.wait_ge(s["windows_ready"], 2)
            pool.wait_ge(s["table_out"], 32)
            pool.memset(big1[:, 0:SW], 0.0).then_inc(s["sums_zero"], 1)
            pool.wait_ge(s["items_ready"], 2)
            fast = pool.value_load(windowed[0:1, 0:1], min_val=0, max_val=1)
            with pool.If(fast > 0):
                with pool.Fori(0, HALF) as i:
                    scatter(i, 0)
                    scatter(i, 1)
            with pool.Else():
                gather(0, 0)
                gather(0, 1)
                with pool.Fori(0, HALF - 1) as i:
                    scatter(i, 0)
                    gather(i + 1, 0)
                    scatter(i, 1)
                    gather(i + 1, 1)
                scatter(HALF - 1, 0)
                scatter(HALF - 1, 1)

            pool.wait_ge(s["early_added"], EARLY)
            def buckets(i):
                return [pool.value_load(item_bkt[0:1, bass.ds(ITEMS + S3 * i + u, 1)], min_val=0, max_val=NB)
                        for u in range(S3)]

            def add_item(i, u, first, b):
                j = S3 * i + u
                pool.wait_ge(s["part_ready"], j + 1)
                if not first or u:
                    pool.wait_ge(s["part_added"], j)
                pool.sem_inc(s["pool_turn"], 1)
                dest = big1[:, bass.ds(b * PW, PW)]
                pool.tensor_tensor(dest, dest, part3[u % 2][:, :], ALU.add).then_inc(s["part_added"], 1)
            for u, b in enumerate(buckets(0)):
                add_item(0, u, True, b)
            with pool.Fori(1, ITEMS // S3) as i:
                for u, b in enumerate(buckets(i)):
                    add_item(i, u, False, b)

        @block.scalar
        def _(act):
            act.wait_ge(s["consts_ready"], 2)
            for u in range(2):
                act.dma_start(w1bd[u * R:(u + 1) * R, u * H:(u + 1) * H], w1t).then_inc(s["consts_in"], 16)
                act.dma_start(w2bd[u * H:(u + 1) * H, u * H:(u + 1) * H], w2t).then_inc(s["consts_in"], 16)
                act.dma_start(b1c[u * H:(u + 1) * H, :], b1).then_inc(s["consts_in"], 16)
                act.dma_start(w2bd[2 * H:2 * H + 1, u * H:(u + 1) * H], b2).then_inc(s["consts_in"], 16)
            act.dma_start(embt_s[:, :], embt).then_inc(s["consts_in"], 16)
            act.dma_start(adwt_s[:, :], adaptwt).then_inc(s["consts_in"], 16)
            act.dma_start(gam[:, :], gamma.partition_broadcast(P)).then_inc(s["gb_in"], 16)
            act.dma_start(bet[:, :], beta.partition_broadcast(P)).then_inc(s["gb_in"], 16)
            act.wait_ge(s["pt_psum"], 1)
            act.activation(pt_s[:, :], bank[1][0:GE, 0:NEL], ACT.Copy).then_inc(s["pt_ready"], 1)
            act.wait_ge(s["at_psum"], 1)
            act.activation(at_s[:, :], bank[1][0:NEL, 128:128 + NEL], ACT.Copy).then_inc(s["at_ready"], 1)
            act.wait_ge(s["dist_clip"], 1)
            act.activation(cutw[:, :], cutw[:, :], ACT.Sin, bias=half_pi[:, :],
                           scale=-math.pi / CUTOFF).then_inc(s["cos_ready"], 1)
            def adapt_rows(i):
                for k in range(ZB):
                    act.wait_ge(s["rows_psum"], ZB * i + k + 1)
                    act.activation(tb[:, bass.ds(i * ZB + k, 1), :, MW:TBL].rearrange("p b k c -> p (b k) c"),
                                   bank[1 + k][:, 0:3 * NEL].rearrange("p (k c) -> p k c", k=3),
                                   ACT.Copy).then_inc(s["rows_ready"], 1)

            act.wait_ge(s["x_in"], 16)

            def split(h, k):
                act.wait_ge(s["left_x_ready"], 2 * h + k + 1)
                first_b, end = HALVES[h]
                act.activation(tb[:, first_b:end, k, 0:MW], xm[:, first_b:end, :], ACT.Copy)\
                    .then_inc(s["split_ready"], 1)
            act.wait_ge(s["digits_ready"], 2)
            for k in range(3):
                split(0, k)
                adapt_rows(k)
            adapt_rows(3)
            act.wait_ge(s["rows_b_ready"], GB)
            for k in range(3):
                split(1, k)
                adapt_rows(ZL + k)

            def group(i, u, first, early=False, first_early=False):
                g = 2 * i + u
                prev = not first or u > 0
                act.wait_ge(s["eat_psum"], g + 1)
                if prev:
                    act.wait_ge(s["hid_psum"], g)
                act.activation(eat_s[:, :], mlp_bank[0:2 * R, :], ACT.Copy).then_inc(s["eat_ready"], 1)
                if early:
                    early_one_hots(g - (GA + 3), 1 - u, first_early)
                act.wait_ge(s["hid_psum"], g + 1)
                if prev:
                    act.wait_ge(s["gate_psum"], g)
                act.activation(hid_s[0:2 * H, :], mlp_bank[0:2 * H, :], ACT.Silu,
                               bias=b1c[:, :]).then_inc(s["hid_ready"], 1)

            def parts(i, u, first):
                g = 2 * i + u
                if not first:
                    act.wait_ge(rec_out[u], 16 * T * i)
                act.activation(rec_t[u][:, :, REC - 1], src_f[:, bass.ds(g * T, T)], ACT.Copy)\
                    .then_inc(s["side_ready"], 1)
                act.wait_ge(s["msg_ready"], g + 1)
                act.activation(rec_b[u][:, :, 0, :], msg_s[:, :, :], ACT.Copy).then_inc(s["part0_ready"], 1)
                act.wait_ge(s["left_ready"], g + 1)
                act.activation(rec_b[u][:, :, 1, :], msg_r[:, :, :], ACT.Copy).then_inc(s["part1_ready"], 1)

            def early_apart(i, u, first):
                m = 2 * i + u - (GA + 2)
                act.wait_ge(early_in[u], 16 * (i - PA))
                if not first or u:
                    act.wait_ge(s["apart_ready"], K3 * m)
                act.activation(rel[:, :], rec3[u][:, :, REC - 1], ACT.Identity,
                               bias=item_low[:, bass.ds(m, 1)], scale=-1.0).then_inc(s["rel_ready"], 1)
                act.wait_ge(s["rel_ready"], m + 1)
                if not first or u:
                    act.wait_ge(s["early_oh_ready"], m)
                for t in range(K3):
                    act.activation(apart[:, t, :], iota_f[:, :], ACT.Abs, bias=rel[:, t:t + 1])\
                        .then_inc(s["apart_ready"], 1)

            def early_one_hots(m, u, first):
                act.wait_ge(s["apart_ready"], K3 * m + K3)
                if not first:
                    act.wait_ge(s["early_psum"], m)
                act.activation(oh3[u][:, :, :], apart[:, :, :], ACT.Relu, bias=ones_f[:, 0:1],
                               scale=-1.0).then_inc(s["early_oh_ready"], 1)

            act.wait_ge(s["hilo_ready"], 1)
            group(0, 0, True)
            group(0, 1, True)
            parts(0, 0, True)
            group(1, 0, False)
            parts(0, 1, True)
            group(1, 1, False)
            parts(1, 0, False)
            with act.Fori(2, PA + 1) as i:
                group(i, 0, False)
                parts(i - 1, 1, False)
                group(i, 1, False)
                parts(i, 0, False)
            group(PA + 1, 0, False)
            parts(PA, 1, False)
            early_apart(PA + 1, 0, True)
            group(PA + 1, 1, False, True, True)
            parts(PA + 1, 0, False)
            early_apart(PA + 1, 1, True)
            with act.Fori(PA + 2, HALF) as i:
                group(i, 0, False, True)
                parts(i - 1, 1, False)
                early_apart(i, 0, False)
                group(i, 1, False, True)
                parts(i, 0, False)
                early_apart(i, 1, False)
            parts(HALF - 1, 1, False)
            early_one_hots(EARLY - 1, 1, False)

            def item(i, u, first, more):
                j = S3 * i + u
                v = u % 2
                if v and more:
                    c = chunk_of(act, ITEMS + j + S3)
                act.wait_ge(s["part_psum"], j + 1)
                if not first or u >= 2:
                    act.wait_ge(s["part_added"], j - 1)
                act.activation(part3[v][:, :], bank[v][:, 0:PW], ACT.Copy).then_inc(s["part_ready"], 1)
                if v and more:
                    load_chunk(act, u, c)
            for u in range(S3):
                item(0, u, True, True)
            with act.Fori(1, ITEMS // S3 - 1) as i:
                for u in range(S3):
                    item(i, u, False, True)
            for u in range(S3):
                item(ITEMS // S3 - 1, u, False, False)
            for n in range(2):
                for h, (first_b, end) in enumerate(HALVES):
                    act.wait_ge(s["centred_ready"], 2 * n + h + 1)
                    act.activation(sq[:, first_b:end], y1[:, first_b:end], ACT.Square).then_inc(s["sq_ready"], 1)
                act.wait_ge(s["var_ready"], n + 1)
                act.activation(stat[1][:, :], stat[0][:, :], ACT.Sqrt).then_inc(s["std_ready"], 1)

        @block.vector
        def _(dve):
            step = [0]

            def link(ins):
                step[0] += 1
                ins.then_inc(s["dve_step"], 1)
                dve.wait_ge(s["dve_step"], step[0])

            dve.wait_ge(s["src_in"], 16)
            link(nc.vector.tensor_scalar(hi_i[:, :], src_i[:, :], 10, None, ALU.logical_shift_right))
            link(nc.vector.tensor_copy(dig_a, hi_i[:, :]))
            link(nc.vector.tensor_scalar(hi_i[:, :], src_i[:, :], 7, NBL - 1,
                                         ALU.logical_shift_right, ALU.bitwise_and))
            link(nc.vector.tensor_copy(dig_b, hi_i[:, :]))
            for a in range(NA):
                nc.vector.tensor_scalar(oh_a[:, :, a, :], dig_a.rearrange("p (g j) -> p g j", j=J), float(a), None,
                                        ALU.is_equal)\
                    .then_inc(s["hist_in"], 1)
            for b in range(NBL):
                nc.vector.tensor_scalar(oh_b[:, b, :], dig_b, float(b), None, ALU.is_equal)\
                    .then_inc(s["hist_in"], 1)
            dve.wait_ge(s["hist_in"], NA + NBL)
            link(nc.vector.tensor_scalar(hi_i[:, :], src_i[:, :], 7, None, ALU.logical_shift_right))
            nc.vector.tensor_copy(src_f[:, :], src_i[:, :]).then_inc(s["hilo_ready"], 1)
            dve.wait_ge(s["dist_in"], 16)
            nc.vector.tensor_scalar(cutw[:, :], dist[:, :], CUTOFF, None, ALU.min).then_inc(s["dist_clip"], 1)
            dve.wait_ge(s["consts_ready"], 2)
            link(nc.vector.tensor_scalar(row_a[:, 0:1], row_i[:, :], 4, 3,
                                         ALU.logical_shift_right, ALU.logical_shift_left))
            link(nc.vector.tensor_scalar(row_a[:, 1:2], row_i[:, :], J - 1, None, ALU.bitwise_and))
            link(nc.vector.tensor_copy(row_af[:, :], row_a[:, :]))
            link(nc.vector.tensor_scalar(under_f[:, :, :], under_f[:, :, :], row_af[:, 0:1], None, ALU.is_gt))
            link(nc.vector.tensor_scalar(same_j[:, :], iota_f[:, 0:J], row_af[:, 1:2], None, ALU.is_equal))
            dve.wait_ge(s["dstg_in"], 16)
            link(nc.vector.tensor_reduce(low_g[:, :], dst_g, AX.X, ALU.min))
            link(nc.vector.tensor_reduce(high_g[:, :], dst_g, AX.X, ALU.max))
            link(nc.vector.tensor_scalar(low_g[:, :], low_g[:, :], float((NB - 1) * P), None, ALU.min))
            link(nc.vector.tensor_tensor(high_g[:, :], high_g[:, :], low_g[:, :], ALU.subtract))
            link(nc.vector.tensor_scalar(fits[:, :], high_g[:, :], float(P), None, ALU.is_lt))
            nc.vector.tensor_tensor(low_dg[:, :, :], over_last(low_g[:, :], GP), over_mid(ident_f[0:GP, 0:GP], GB),
                                    ALU.mult).then_inc(s["low_ready"], 1)
            dve.wait_ge(s["hist_ready"], 2)
            for h in range(2):
                link(nc.vector.tensor_tensor(diag[:, h], hist[h].rearrange("p (b j) -> p b j", b=NBL),
                                             over_mid(same_j[0:NA * J, :], NBL), ALU.mult))
                nc.vector.reduce_sum(digits[:, h, :], diag[:, h], axis=AX.X).then_inc(s["digits_ready"], 1)

            def types(i):
                nc.vector.tensor_scalar(zoh[:, i * ZB * P:(i + 1) * ZB * P], zrow_i[:, i * ZB * P:(i + 1) * ZB * P],
                                        iota_p[0:NEL, :], None, ALU.is_equal).then_inc(s["zoh_ready"], 1)

            def left_x(h, k):
                dve.wait_ge(s["split_ready"], 3 * h + k + 1)
                first_b, end = HALVES[h]
                nc.vector.tensor_tensor(xm[:, first_b:end, :], xm[:, first_b:end, :],
                                        tb[:, first_b:end, k, 0:MW], ALU.subtract)\
                    .then_inc(s["left_x_ready"], 1)
            dve.wait_ge(s["zrow_in"], 16)
            dve.wait_ge(s["z_in"], 32)
            nc.vector.tensor_copy(xm[:, :, H], mult_s[:, :]).then_inc(s["left_x_ready"], 1)
            types(0)
            dve.wait_ge(s["at_ready"], 1)
            link(nc.vector.tensor_copy(at3[:, 0, :], at_s[:, :]))
            link(nc.vector.tensor_tensor(at_r[:, :], at_s[:, :], at3[:, 0, :], ALU.subtract))
            link(nc.vector.tensor_copy(at3[:, 1, :], at_r[:, :]))
            link(nc.vector.tensor_tensor(at_r[:, :], at_r[:, :], at3[:, 1, :], ALU.subtract))
            nc.vector.tensor_copy(at3[:, 2, :], at_r[:, :]).then_inc(s["at3_ready"], 1)
            types(1)
            dve.wait_ge(s["base_psum"], 1)
            for h in range(2):
                nc.vector.tensor_scalar(starts[:, h, :], bank[0][:, 256 + 64 * h:256 + 64 * h + NB + 1],
                                        float(STARTS[h] * P * T), None, ALU.add).then_inc(s["base_read"], 1)
            left_x(0, 0)
            types(2)
            dve.wait_ge(s["base_read"], 2)
            link(nc.vector.tensor_copy(starts_i[:, :, :], starts[:, :, :]))
            link(nc.vector.tensor_copy(base[:, :], starts[:, 0, 0:NB]))
            dve.wait_ge(s["low_psum"], 1)
            link(nc.vector.reduce_sum(fit_all[:, 0:1], bank[0][:, 0:GB], axis=AX.X))
            link(nc.vector.tensor_scalar(fit_all[:, 1:2], fit_all[:, 0:1], G - 0.5, None, ALU.is_gt))
            nc.vector.tensor_copy(low_i[:, :], bank[0][0:1, 64:64 + G]).then_inc(s["windows_ready"], 1)
            nc.vector.tensor_copy(windowed[:, :], fit_all[0:1, 1:2]).then_inc(s["windows_ready"], 1)
            left_x(0, 1)
            types(3)
            dve.wait_ge(s["srcg_in"], 16)
            link(nc.vector.tensor_scalar(src_g, src_g, P - 1, None, ALU.bitwise_and))
            link(nc.vector.tensor_copy(rows_b[:, :, 0, :], src_g))
            for b in range(GB):
                link(nc.vector.scalar_tensor_tensor(loc_g[:, b, :], dst_g[:, b, :], low_g[:, b:b + 1],
                                                    own_row, ALU.subtract, ALU.subtract))
                nc.vector.scalar_tensor_tensor(rows_b[:, b, 1, :], loc_g[:, b, :], fit_all[0:GP, 1:2],
                                               own_row, ALU.mult, ALU.add).then_inc(s["rows_b_ready"], 1)
            types(ZL)
            types(ZL + 1)
            left_x(1, 0)
            types(ZL + 2)
            nc.vector.tensor_scalar(z_b[:, :], z_i[:, :], float(-ZBIAS), float(1 << ZSHIFT), ALU.add, ALU.mult)\
                .then_inc(s["zb_ready"], 1)
            dve.wait_ge(s["cos_ready"], 1)
            link(nc.vector.tensor_scalar(cutw[:, :], cutw[:, :], 1.0, 0.5, ALU.add, ALU.mult))
            nc.vector.scalar_tensor_tensor(cutw[:, :], dist[:, :], CUTOFF, cutw[:, :],
                                           ALU.is_lt, ALU.mult).then_inc(s["cutw_ready"], 1)
            left_x(1, 1)
            for h in range(2):
                link(nc.vector.tensor_scalar(chunk_i[:, :], starts_i[:, h, 0:NB], CSHIFT, None, ALU.arith_shift_right))
                link(nc.vector.tensor_scalar(first_c[:, :], chunk_i[:, :], float(STARTS[h + 1] - 1), None, ALU.min))
                link(nc.vector.tensor_scalar(chunk_f[:, :], starts[:, h, 1:NB + 1], -1.0, None, ALU.add))
                link(nc.vector.tensor_copy(chunk_i[:, :], chunk_f[:, :]))
                link(nc.vector.tensor_scalar(chunk_i[:, :], chunk_i[:, :], CSHIFT, None, ALU.arith_shift_right))
                link(nc.vector.tensor_copy(chunk_f[:, :], chunk_i[:, :]))
                link(nc.vector.tensor_tensor(last_c[:, :], chunk_f[:, :], first_c[:, :], ALU.max))
                link(nc.vector.tensor_tensor(last_c[:, :], last_c[:, :], first_c[:, :], ALU.subtract))
                link(nc.vector.tensor_scalar(last_c[:, :], last_c[:, :], 1.0, None, ALU.add))
                link(nc.vector.tensor_tensor_scan(ends[:, :], ones_f[:, 0:NB], last_c[:, :], 0.0, ALU.mult, ALU.add))
                link(nc.vector.tensor_tensor(chunk_f[:, :], last_c[:, :], ends[:, :], ALU.subtract))
                link(nc.vector.tensor_tensor(first_c[:, :], first_c[:, :], chunk_f[:, :], ALU.add))
                link(nc.vector.memset(shift[:, :], 0.0))
                link(nc.vector.tensor_tensor(shift[:, 0:NB - 1], first_c[:, 1:NB], first_c[:, 0:NB - 1],
                                             ALU.subtract))
                link(nc.vector.tensor_tensor(past[:, :, :], over_mid(ends[:, :], IB), over_last(item_no[:, :], NB),
                                             ALU.is_le))
                link(nc.vector.tensor_tensor(past_d[:, :, :], past[:, :, :], over_mid(shift[:, 0:NB], IB), ALU.mult))
                link(nc.vector.reduce_sum(item_v[:, 0, :], past[:, :, :], axis=AX.X))
                link(nc.vector.reduce_sum(item_v[:, 1, :], past_d[:, :, :], axis=AX.X))
                link(nc.vector.tensor_tensor(item_v[:, 1, :], item_v[:, 1, :], item_no[:, :], ALU.add))
                link(nc.vector.tensor_scalar(item_v[:, 1, :], item_v[:, 1, :], float(STARTS[h]),
                                             float(STARTS[h + 1] - 1), ALU.add, ALU.min))
                for w in range(2):
                    nc.vector.tensor_tensor(item_dg[:, w, h], over_last(item_v[0:IP, w, :], IP),
                                            over_mid(ident_f[0:IP, 0:IP], IB), ALU.mult).then_inc(s["items_diag"], 1)
                dve.wait_ge(s["items_diag"], 2 * h + 2)
            dve.wait_ge(s["item_psum"], 2)
            link(nc.vector.tensor_scalar(item_low[:, :], bank[6][:, 0:2 * ITEMS], float(P), None, ALU.mult))
            nc.vector.tensor_copy(item_bkt[:, :], bank[6][0:1, 0:2 * ITEMS]).then_inc(s["items_ready"], 1)
            nc.vector.tensor_copy(item_chk[:, :], bank[7][0:1, 0:2 * ITEMS]).then_inc(s["items_ready"], 1)

            dve.wait_ge(s["cutw_ready"], 1)

            def one_hots(g, i, u, again):
                if again:
                    dve.wait_ge(s["place_psum"], g - 1)
                nc.vector.tensor_tensor(oh_hi[u][:, :, :], over_last(hi_i[:, bass.ds(g * T, T)], NB),
                                        over_mid(iota_f[:, 0:NB], T), ALU.is_equal).then_inc(s["hi_ready"], 1)
                dve.wait_ge(row_in[u], 16 * i + 16)
                if again:
                    dve.wait_ge(s["win_psum"], g - 1)
                nc.vector.tensor_scalar(oht[u].rearrange("p k e -> p (k e)"), row_t[u], iota_p[:, :], None,
                                        ALU.is_equal).then_inc(s["oht_ready"], 1)

            def pick(g, u):
                dve.wait_ge(s["hi_ready"], g + 1)
                dve.wait_ge(s["place_psum"], g + 1)
                nc.vector.tensor_tensor(picked[:, :, :], place_bank, oh_hi[u][:, :, :], ALU.mult)\
                    .then_inc(s["place_picked"], 1)

            def places(g, part_ends=False):
                if part_ends:
                    nc.vector.tensor_copy(base[:, :], starts[:, 1, 0:NB]).then_inc(s["base_moved"], 1)
                else:
                    nc.vector.tensor_tensor(base[:, :], base[:, :], count_bank, ALU.add)\
                        .then_inc(s["base_moved"], 1)
                dve.wait_ge(s["place_picked"], g + 1)
                nc.vector.reduce_sum(place_f[:, :], picked[:, :, :], axis=AX.X).then_inc(s["place_f_ready"], 1)

            def pos_out(g, i, u, again):
                dve.wait_ge(s["place_i_ready"], g + 1)
                if again:
                    dve.wait_ge(rec_out[u], 16 * T * i)
                nc.vector.tensor_scalar(pos_t[u][:, :].bitcast(i32), place_i[:, :], (1 << ZSHIFT) - 1, None,
                                        ALU.bitwise_and).then_inc(s["pos_ready"], 1)

            def places_out(g, prev):
                dve.wait_ge(s["place_f_ready"], g + 1)
                if prev:
                    dve.wait_ge(s["pos_ready"], g)
                nc.vector.tensor_copy(place_i[:, :], place_f[:, :]).then_inc(s["place_i_ready"], 1)
                dve.wait_ge(s["place_i_ready"], g + 1)
                nc.vector.tensor_scalar(z_edge[:, :], place_i[:, :], ZSHIFT, None, ALU.arith_shift_right)\
                    .then_inc(s["z_ready"], 1)
                dve.wait_ge(s["z_ready"], g + 1)
                nc.vector.tensor_scalar(zs[:, :], z_edge[:, :], float(ZBIAS), None, ALU.add)\
                    .then_inc(s["zs_ready"], 1)

            def early_add(m, b, prev=True):
                dve.wait_ge(s["early_psum"], m + 1)
                if prev:
                    dve.wait_ge(s["early_added"], m)
                dest = big1[:, bass.ds(b * PW, PW)]
                dve.sem_inc(s["dve_turn"], 1)
                nc.vector.tensor_tensor(dest, dest, bank[6][:, 0:PW], ALU.add).then_inc(s["early_added"], 1)

            def bucket_of(m):
                return dve.value_load(item_bkt[0:1, bass.ds(m, 1)], min_val=0, max_val=NB)

            def two(ap):
                return ap.rearrange("p (k t) c -> p k t c", t=2)

            def message(g, i, u, early=0):
                dve.wait_ge(s["win_psum"], g + 1)
                nc.vector.tensor_copy(two(msg_s[:, :, H:MW]), win_bank[:, :, :, H:MW]).then_inc(s["wm_ready"], 1)
                dve.wait_ge(s["zs_ready"], g + 1)
                for t in range(T):
                    nc.vector.scalar_tensor_tensor(junk[:, t, :], iota_f[:, 0:NEL], zs[:, t:t + 1],
                                                   win_bank[:, t // 2, t % 2, MW:TBL], ALU.is_equal, ALU.mult,
                                                   accum_out=adapt[:, t:t + 1]).then_inc(s["adapt_ready"], 1)
                if early:
                    m = g - (GA + 3)
                    early_add(m, bucket_of(m), early > 1)
                dve.wait_ge(s["wm_ready"], 2 * g + 1)
                nc.vector.tensor_tensor(wm[:, :], msg_s[:, :, H], cutw[:, bass.ds(g * T, T)], ALU.mult)\
                    .then_inc(s["wm_ready"], 1)
                dve.wait_ge(s["gate_psum"], g + 1)
                dve.wait_ge(s["adapt_ready"], T * g + T)
                nc.vector.tensor_tensor(gate_s[:, :, :], gate_bank, over_last(adapt[:, :], H), ALU.add)\
                    .then_inc(s["gate_ready"], 1)
                dve.wait_ge(s["wm_ready"], 2 * g + 2)
                nc.vector.tensor_tensor(two(wh_s[:, :, :]), win_bank[:, :, :, 0:H],
                                        two(over_last(wm[:, :], H)), ALU.mult).then_inc(s["wh_ready"], 1)

            def message_out(g):
                dve.wait_ge(s["gate_ready"], g + 1)
                dve.wait_ge(s["wh_ready"], g + 1)
                nc.vector.tensor_tensor(msg_s[:, :, 0:H], gate_s[:, :, :], wh_s[:, :, :], ALU.mult)\
                    .then_inc(s["msg_ready"], 1)

            def left(g, u):
                dve.wait_ge(s["part0_ready"], g + 1)
                dve.wait_ge(s["msg_ready"], g + 1)
                nc.vector.tensor_tensor(msg_r[:, :, :], msg_s[:, :, :], rec_b[u][:, :, 0, :], ALU.subtract)\
                    .then_inc(s["left_ready"], 1)

            def last_part(g, u):
                dve.wait_ge(s["part1_ready"], g + 1)
                dve.wait_ge(s["left_ready"], g + 1)
                nc.vector.tensor_tensor(rec_b[u][:, :, 2, :], msg_r[:, :, :], rec_b[u][:, :, 1, :], ALU.subtract)\
                    .then_inc(s["rec_ready"], 1)

            def turn(i, u, slot_used=True, one_hots_too=True, part_ends=False, early=0):
                g, n, nu = 2 * i + u, 2 * i + u + 1, 1 - u
                if one_hots_too:
                    one_hots(g + 2, i + 1, u, True)
                message(g, i, u, early)
                pick(n, nu)
                message_out(g)
                places(n, part_ends)
                pos_out(g, i, u, slot_used)
                left(g, u)
                places_out(n, True)
                last_part(g, u)

            one_hots(0, 0, 0, False)
            one_hots(1, 0, 1, False)
            pick(0, 0)
            places(0)
            places_out(0, False)
            turn(0, 0, False)
            turn(0, 1, False)
            with dve.Fori(1, PA - 1) as i:
                turn(i, 0)
                turn(i, 1)
            turn(PA - 1, 0, part_ends=True)
            turn(PA - 1, 1)
            turn(PA, 0)
            turn(PA, 1)
            dve.wait_ge(s["sums_zero"], 1)
            turn(PA + 1, 0)
            turn(PA + 1, 1, early=1)
            with dve.Fori(PA + 2, HALF - 1) as i:
                turn(i, 0, early=2)
                turn(i, 1, early=2)
            turn(HALF - 1, 0, one_hots_too=False, early=2)
            message(G - 1, HALF - 1, 1, 2)
            message_out(G - 1)
            pos_out(G - 1, HALF - 1, 1, True)
            left(G - 1, 1)
            last_part(G - 1, 1)
            early_add(EARLY - 1, bucket_of(EARLY - 1))

            dve.wait_ge(s["win_psum"], G)
            dve.wait_ge(s["xn_in"], 16)
            dve.wait_ge(s["gb_in"], 32)
            link(nc.vector.tensor_tensor(xb, xn, over_mid(bet[:, :], NB), ALU.add))

            def item(i, u, first):
                j = S3 * i + u
                v = u % 2
                dve.wait_ge(rec3_in[u], 16 * i + 16)
                if not first or u >= 2:
                    dve.wait_ge(s["part_psum"], j - 1)
                nc.vector.scalar_tensor_tensor(oh3[v][:, :, :], over_mid(iota_f[:, :], K3),
                                               item_low[:, bass.ds(ITEMS + j, 1)],
                                               over_last(rec3[u][:, :, REC - 1], P), ALU.add, ALU.is_equal).then_inc(s["oh3_ready"], 1)
            for u in range(S3):
                item(0, u, True)
            with dve.Fori(1, ITEMS // S3) as i:
                for u in range(S3):
                    item(i, u, False)

            dve.wait_ge(s["part_added"], ITEMS)
            whole = sums[:, 0:NB, 0, :]
            for k in (1, 2):
                link(nc.vector.tensor_tensor(whole, whole, sums[:, 0:NB, k, :], ALU.add))
            link(nc.vector.tensor_scalar(stat[0][:, :], whole[:, :, H], 1e-8, None, ALU.max))
            link(nc.vector.reciprocal(stat[1][:, :], stat[0][:, :]))
            link(nc.vector.tensor_tensor(y1, whole[:, :, 0:H], over_last(stat[1][:, :], H), ALU.mult))
            link(nc.vector.tensor_tensor(y1, y1, xn, ALU.add))

            def norm(y, n):
                link(nc.vector.reduce_sum(stat[0][:, :], y, axis=AX.X))
                link(nc.vector.tensor_scalar(stat[0][:, :], stat[0][:, :], 1.0 / H, None, ALU.mult))
                for first_b, end in HALVES:
                    nc.vector.tensor_tensor(y[:, first_b:end], y[:, first_b:end],
                                            over_last(stat[0][:, first_b:end], H),
                                            ALU.subtract).then_inc(s["centred_ready"], 1)
                for h, (first_b, end) in enumerate(HALVES):
                    dve.wait_ge(s["centred_ready"], 2 * n + 2)
                    dve.wait_ge(s["sq_ready"], 2 * n + h + 1)
                    link(nc.vector.reduce_sum(stat[0][:, first_b:end], sq[:, first_b:end], axis=AX.X))
                nc.vector.tensor_scalar(stat[0][:, :], stat[0][:, :], 1.0 / H, EPS, ALU.mult, ALU.add)\
                    .then_inc(s["var_ready"], 1)
                dve.wait_ge(s["std_ready"], n + 1)
                link(nc.vector.reciprocal(stat[0][:, :], stat[1][:, :]))
            norm(y1, 0)
            link(nc.vector.tensor_tensor(y1, y1, over_last(stat[0][:, :], H), ALU.mult))
            link(nc.vector.tensor_tensor(y1, y1, over_mid(gam[:, :], NB), ALU.mult))
            link(nc.vector.tensor_tensor(y1, y1, xb, ALU.add))
            norm(y1, 1)
            for first_b, end in HALVES:
                nc.vector.tensor_tensor(y2[:, first_b:end], y1[:, first_b:end],
                                        over_last(stat[0][:, first_b:end], H), ALU.mult)\
                    .then_inc(s["y_ready"], 1)

        @block.tensor
        def _(pe):
            pe.wait_ge(s["hist_in"], NA + NBL)

            def count(h, c, start, stop):
                return nc.tensor.matmul(hist[h], oh_a[:, c].rearrange("p a j -> p (a j)"),
                                        oh_b[:, :, c * J:(c + 1) * J],
                                        start=start, stop=stop)
            for h in range(2):
                first, stop = STARTS[h] * T // J, STARTS[h + 1] * T // J
                for c in range(first, stop):
                    last = count(h, c, c == first, c == stop - 1)
                last.then_inc(s["hist_ready"], 1)
            pe.wait_ge(s["consts_in"], 16 * 10)
            nc.tensor.matmul(bank[1][0:GE, 0:NEL], adwt_s[:, :], embt_s[:, :], start=True, stop=True)\
                .then_inc(s["pt_psum"], 1)
            pe.wait_ge(s["pt_ready"], 1)
            nc.tensor.matmul(bank[1][0:NEL, 128:128 + NEL], pt_s[:, :], embt_s[:, :], start=True, stop=True)\
                .then_inc(s["at_psum"], 1)
            pe.wait_ge(s["digits_ready"], 2)
            for h in range(2):
                for b in range(NBL):
                    last = nc.tensor.matmul(bank[0][:, 256 + 64 * h:256 + 64 * h + NB + 1],
                                            digits[:, h, b:b + 1].to_broadcast([NA * J, P]),
                                            under_f[0:NA * J, b, :], start=b == 0, stop=b == NBL - 1)
            last.then_inc(s["base_psum"], 1)
            pe.wait_ge(s["low_ready"], 1)
            pe.wait_ge(s["base_read"], 2)
            nc.tensor.matmul(bank[0][:, 0:GB], ones_f[0:GP, :], fits[:, :], start=True, stop=True)
            nc.tensor.matmul(bank[0][:, 64:64 + G], ones_f[0:GP, :], low_dg[:, :, :], start=True, stop=True)\
                .then_inc(s["low_psum"], 1)
            pe.wait_ge(s["at3_ready"], 1)

            def types(i, first):
                pe.wait_ge(s["zoh_ready"], i + 1)
                for k in range(ZB):
                    if not first:
                        pe.wait_ge(s["rows_ready"], ZB * i + k - ZB + 1)
                    nc.tensor.matmul(bank[1 + k][:, 0:3 * NEL], zoh[:, bass.ds(i * (ZB * P) + k * P, P)],
                                     at3[:, :, :].rearrange("z k c -> z (k c)"), start=True, stop=True)\
                        .then_inc(s["rows_psum"], 1)
            types(0, True)
            with pe.Fori(1, NB // ZB) as i:
                types(i, False)
            pe.wait_ge(s["rows_ready"], NB)
            for w in range(2):
                pe.wait_ge(s["items_diag"], w + 3)
                nc.tensor.matmul(bank[6 + w][:, 0:2 * ITEMS], ones_f[0:IP, :],
                                 item_dg[:, w].rearrange("p h b c -> p (h b c)"), start=True, stop=True)\
                    .then_inc(s["item_psum"], 1)
            pe.wait_ge(s["items_ready"], 2)
            pe.wait_ge(s["windows_ready"], 2)
            pe.wait_ge(s["zb_ready"], 1)

            def early_item(m, u, prev=True):
                pe.wait_ge(s["early_oh_ready"], m + 1)
                if prev:
                    pe.wait_ge(s["early_added"], m)
                for t in range(K3):
                    last = nc.tensor.matmul(bank[6][:, 0:PW], oh3[u][:, t, :],
                                            rec3[u][:, t, :].bitcast(bf16)[:, 0:PW],
                                            start=t == 0, stop=t == K3 - 1)
                last.then_inc(s["early_psum"], 1)

            def group(i, u, first, windowed, early=None, early_prev=True):
                g = 2 * i + u
                prev = not first or u > 0
                pe.wait_ge(ea_in[u], 16 * i + 16)
                if prev:
                    pe.wait_ge(s["hid_ready"], g)
                for k in range(T // 2):
                    last = nc.tensor.transpose(mlp_bank[0:2 * R, k * P:(k + 1) * P],
                                               ea_t[u][:, 2 * R * k:2 * R * (k + 1)], ident_f[:, :])
                last.then_inc(s["eat_psum"], 1)
                pe.wait_ge(s["hi_ready"], g + 1)
                if prev:
                    pe.wait_ge(s["base_moved"], g)
                nc.tensor.matmul(place_bank, ident_f[:, :], over_mid(base[:, 0:NB], T), start=True, stop=False,
                                 skip_group_check=True)
                nc.tensor.matmul(place_bank, before_b[:, :], oh_hi[u][:, :, :], start=False, stop=False,
                                 skip_group_check=True)
                for t in range(T - 1):
                    nc.tensor.matmul(place_bank[:, t + 1:T, :], ones_b[:, :],
                                     over_mid(oh_hi[u][:, t, :], T - 1 - t), start=False, stop=False,
                                     skip_group_check=True)
                pe.wait_ge(s["oht_ready"], g + 1)
                for t in range(T):
                    nc.tensor.matmul(place_bank[:, t, :], oht[u][:, 0, t::T], z_b[:, :],
                                     start=False, stop=True, skip_group_check=True)
                for t in range(T):
                    last = nc.tensor.matmul(count_bank, ones_b[:, :], oh_hi[u][:, t, :],
                                            start=t == 0, stop=t == T - 1)
                last.then_inc(s["place_psum"], 1)
                pe.wait_ge(s["eat_ready"], g + 1)
                nc.tensor.matmul(mlp_bank[0:2 * H, :], w1bd[:, :], eat_s[:, :], start=True, stop=True)\
                    .then_inc(s["hid_psum"], 1)
                if early is not None:
                    early_item(early, 1 - u, early_prev)
                if windowed:
                    pe.wait_ge(win_in[u], 16 * i + 16)
                else:
                    pe.wait_ge(rows_in[u], 16 * T * (i + 1))
                if prev:
                    pe.wait_ge(s["wh_ready"], g)
                for t in range(T):
                    for k in range(3):
                        last = nc.tensor.matmul(win_bank[:, t // 2, t % 2, :], oht[u][:, 1, t::T],
                                                win_t[u][:, 0 if windowed else t, k * TBL:(k + 1) * TBL],
                                                start=k == 0, stop=k == 2)
                last.then_inc(s["win_psum"], 1)
                pe.wait_ge(s["hid_ready"], g + 1)
                if prev:
                    pe.wait_ge(s["gate_ready"], g)
                for k in range(T // 2):
                    last = nc.tensor.matmul(gate_psum[:, 2 * H * k:2 * H * (k + 1)], hid_s[:, k * P:(k + 1) * P],
                                            w2bd[:, :], start=True, stop=True)
                last.then_inc(s["gate_psum"], 1)

            def groups(windowed):
                group(0, 0, True, windowed)
                group(0, 1, True, windowed)
                with pe.Fori(1, PA + 1) as i:
                    group(i, 0, False, windowed)
                    group(i, 1, False, windowed)
                group(PA + 1, 0, False, windowed)
                group(PA + 1, 1, False, windowed, 0, False)
                with pe.Fori(PA + 2, HALF) as i:
                    group(i, 0, False, windowed, 2 * i - (GA + 3))
                    group(i, 1, False, windowed, 2 * i - (GA + 2))
            fast = pe.value_load(windowed[0:1, 0:1], min_val=0, max_val=1)
            with pe.If(fast > 0):
                groups(True)
            with pe.Else():
                groups(False)
            early_item(EARLY - 1, 1)

            def item(i, u, first):
                j = S3 * i + u
                v = u % 2
                pe.wait_ge(s["oh3_ready"], j + 1)
                if not first or u >= 2:
                    pe.wait_ge(s["part_ready"], j - 1)
                for t in range(K3):
                    last = nc.tensor.matmul(bank[v][:, 0:PW], oh3[v][:, t, :],
                                            rec3[u][:, t, :].bitcast(bf16)[:, 0:PW],
                                            start=t == 0, stop=t == K3 - 1)
                last.then_inc(s["part_psum"], 1)
            for u in range(S3):
                item(0, u, True)
            with pe.Fori(1, ITEMS // S3) as i:
                for u in range(S3):
                    item(i, u, False)


def kernel(x, src, dst, edge_attr_40, edge_weight, node_type_119, node_vec, L0_gnn_W1, L0_gnn_b1,
           L0_gnn_W2, L0_gnn_b2, L0_gnn_emb, L0_gnn_adaptW, L0_gnn_gamma, L0_gnn_beta):
    import numpy as np
    import concourse.bacc as bacc
    from concourse.bass_utils import run_bass_kernel_spmd as run

    nc = bacc.Bacc("TRN2", target_bir_lowering=False, num_devices=1)
    pad = EP - E
    npad = NB * P - N

    def edges(a, fill):
        a = np.concatenate([np.asarray(a), np.full((pad,), fill, a.dtype)])
        return np.ascontiguousarray(a.reshape(G, P, T).transpose(1, 0, 2).reshape(P, C))

    def nodes(a):
        return np.ascontiguousarray(np.concatenate([np.asarray(a), np.zeros((npad,), a.dtype)]))

    arrays = {
        "in_x": np.concatenate([np.asarray(x), np.zeros((npad, H), np.float32)]),
        "in_src": edges(src, NB * P - 1),
        "in_src_rows": np.concatenate([np.asarray(src), np.full((pad,), NB * P - 1, np.int32)]).reshape(G * P, T),
        "in_dst": np.concatenate([np.asarray(dst), np.full((pad,), N - 1, np.int32)]).reshape(G * P, T),
        "in_weight": edges(edge_weight, 0),
        "in_ea": np.concatenate([np.asarray(edge_attr_40), np.zeros((pad, R), np.float32)]).reshape(G * P, T * R),
        "in_z_nodes": np.ascontiguousarray(nodes(node_type_119).reshape(NB, P).T),
        "in_z_row": nodes(node_type_119),
        "in_mult": np.ascontiguousarray(nodes(node_vec).reshape(NB, P).T),
        "in_w1t": np.ascontiguousarray(np.asarray(L0_gnn_W1).T),
        "in_b1": np.asarray(L0_gnn_b1).reshape(H, 1),
        "in_w2t": np.ascontiguousarray(np.asarray(L0_gnn_W2).T),
        "in_b2": np.asarray(L0_gnn_b2).reshape(1, H),
        "in_embt": np.ascontiguousarray(np.asarray(L0_gnn_emb).T),
        "in_adaptwt": np.ascontiguousarray(np.asarray(L0_gnn_adaptW).T),
        "in_gamma": np.asarray(L0_gnn_gamma),
        "in_beta": np.asarray(L0_gnn_beta),
    }
    args = []
    for name, a in arrays.items():
        dt = mybir.dt.from_np(a.dtype)
        if name == "in_dst":
            dt = mybir.dt.uint32
            arrays[name] = a.view(np.uint32)
        args.append(nc.dram_tensor(name, a.shape, dt, kind="ExternalInput").ap())
    args.append(nc.dram_tensor("node_table", (NB * P, 3 * TBL), mybir.dt.bfloat16, kind="Internal").ap())
    args.append(nc.dram_tensor("node_rows", (G, 2 * P * T), mybir.dt.bfloat16, kind="Internal").ap())
    args.append(nc.dram_tensor("sorted_rec", (EP, REC), mybir.dt.float32, kind="Internal").ap())
    args.append(nc.dram_tensor("out", (N, H), mybir.dt.float32, kind="ExternalOutput").ap())
    build(nc, *args)
    return run(nc, [arrays], core_ids=[0]).results[0]["out"]
```
